# Optimizing a Trainium2 kernel written in Bass

```python
import numpy as np
import jax
import jax.numpy as jnp

def _softmax(x, axis=-1):
    return jax.nn.softmax(x, axis=axis)

def _gelu(x):
    return jax.nn.gelu(x, approximate=True)

def _silu(x):
    return jax.nn.silu(x)

def _sigmoid(x):
    return jax.nn.sigmoid(x)

def _layernorm(x, axis=-1, eps=1e-05):
    m = jnp.mean(x, axis=axis, keepdims=True)
    v = jnp.var(x, axis=axis, keepdims=True)
    return (x - m) / jnp.sqrt(v + eps)

def _scatter_add(tgt, idx, src, axis=0):
    return tgt.at[idx].add(src)

def _segment_sum(src, seg, n):
    return jax.ops.segment_sum(src, seg, n)
kernel_name = 'mk_adaln_attn_ffn_d1_seqx_r8_5a3939'

def setup_inputs(seed: int=0):
    np.random.seed(seed)
    _w = jnp.asarray

    def _rec_inputs():
        import jax
        import jax.numpy as jnp
        _rk = jax.random.key(seed)
        x = -7.109e-05 + 0.9999 * jax.random.normal(jax.random.fold_in(_rk, 1), (32, 32, 512), jnp.float32)
        _lenS = 32 - jax.random.randint(jax.random.fold_in(_rk, 7), (32,), 0, max(1, 32 // 4) + 1, jnp.int32)
        _lenS2 = 32 - jax.random.randint(jax.random.fold_in(_rk, 8), (32,), 0, max(1, 32 // 4) + 1, jnp.int32)
        itok_B_0_30 = jax.random.randint(jax.random.fold_in(_rk, 11), (32,), 0, 31, jnp.int32)
        itok_B_0_7 = jax.random.randint(jax.random.fold_in(_rk, 12), (32,), 0, 8, jnp.int32)
        return (x, itok_B_0_30, itok_B_0_7)
    x, itok_B_0_30, itok_B_0_7 = _rec_inputs()

    def _L0_cond_setup():
        import jax, jax.numpy as jnp
        import numpy as np
        B, C, D, T, S = (64, 32, 32, 512, 32)
        key = jax.random.key(seed)
        k1, k2, k3 = jax.random.split(key, 3)
        x = jax.random.normal(k1, (B, C, T), dtype=jnp.float32)
        subjects = jax.random.randint(k2, (B,), 0, S, dtype=jnp.int64)
        weights = jax.random.normal(k3, (S, C, D), dtype=jnp.float32) * (1.0 / np.sqrt(C))
        return {'x': x, 'subjects': subjects, 'weights': weights}
    _L0_cond_all = _L0_cond_setup()
    _L0_cond_in = {k: v for k, v in _L0_cond_all.items() if k in ('weights',)}
    del _L0_cond_all

    def _L0_attn_setup():
        import math
        import jax, jax.numpy as jnp
        import numpy as np

        def _rope_tables(T, h, dtype):
            pos = jnp.arange(T, dtype=jnp.float32)
            thetas = 1.0 / 10000.0 ** (jnp.arange(0, h, 2, dtype=jnp.float32) / h)
            pt = jnp.outer(pos, thetas)
            pt = jnp.concatenate([pt, pt], axis=-1)
            return (jnp.sin(pt).astype(dtype), jnp.cos(pt).astype(dtype))

        def _apply_rope(x, sin, cos):
            h = x.shape[-1]
            rot = jnp.concatenate([-x[..., h // 2:], x[..., :h // 2]], axis=-1)
            return x * cos + rot * sin
        key = jax.random.key(seed)
        ks = jax.random.split(key, 5)
        B, T, C = (2, 256, 512)
        s = 1.0 / math.sqrt(C)
        return {'x': jax.random.normal(ks[0], (B, T, C), dtype=jnp.float32), 'wq': jax.random.normal(ks[1], (C, C), dtype=jnp.float32) * s, 'wk': jax.random.normal(ks[2], (C, C), dtype=jnp.float32) * s, 'wv': jax.random.normal(ks[3], (C, C), dtype=jnp.float32) * s, 'wo': jax.random.normal(ks[4], (C, C), dtype=jnp.float32) * s}
    _L0_attn_all = _L0_attn_setup()
    _L0_attn_in = {k: v for k, v in _L0_attn_all.items() if k in ('wq', 'wk', 'wv', 'wo')}
    del _L0_attn_all

    def _L0_cond2_setup():
        import jax, jax.numpy as jnp
        import numpy as np
        TOP_K = 2
        LANG_BIAS = 5.0
        SCALING = 32.0 / 16.0
        LANGUAGE_PAD_ID = -1
        key = jax.random.key(seed)
        ks = jax.random.split(key, 6)
        B, T, D, O, E, R = (4, 256, 512, 512, 8, 16)
        x = jax.random.normal(ks[0], (B, T, D), dtype=jnp.float32)
        language_ids = jax.random.randint(ks[1], (B,), 0, E).astype(jnp.int64)
        W = jax.random.normal(ks[2], (O, D), dtype=jnp.float32) * (1.0 / np.sqrt(D))
        Wr = jax.random.normal(ks[3], (E, D), dtype=jnp.float32) * (1.0 / np.sqrt(D))
        A = jax.random.normal(ks[4], (E, R, D), dtype=jnp.float32) * (1.0 / np.sqrt(D))
        Bm = jax.random.normal(ks[5], (O, R), dtype=jnp.float32) * 0.0
        Bm = jnp.broadcast_to(Bm, (E, O, R)) + jax.random.normal(ks[5], (E, O, R), dtype=jnp.float32) * 0.02
        return {'x': x, 'language_ids': language_ids, 'W': W, 'Wr': Wr, 'A': A, 'B': Bm}
    _L0_cond2_all = _L0_cond2_setup()
    _L0_cond2_in = {k: v for k, v in _L0_cond2_all.items() if k in ('W', 'Wr', 'A', 'B')}
    del _L0_cond2_all

    def _L0_ffn_setup():
        import jax, jax.numpy as jnp
        import numpy as np
        B, L, H, Dh, M = (4, 256, 16, 32, 128)
        D = H * Dh
        key = jax.random.key(seed)
        kx, ku, kd, kp = jax.random.split(key, 4)
        x = jax.random.normal(kx, (B, L, D), dtype=jnp.float32)
        up = jax.random.normal(ku, (H, Dh, M), dtype=jnp.float32)
        down = jax.random.normal(kd, (H, M, Dh), dtype=jnp.float32)
        perm = jax.random.permutation(kp, D)
        return {'x': x, 'up': up, 'down': down, 'perm': perm}
    _L0_ffn_all = _L0_ffn_setup()
    _L0_ffn_in = {k: v for k, v in _L0_ffn_all.items() if k in ('up', 'down', 'perm')}
    del _L0_ffn_all
    return {'x': x, 'itok_B_0_30': itok_B_0_30, 'itok_B_0_7': itok_B_0_7, 'L0_cond_weights': _L0_cond_in['weights'], 'L0_attn_wq': _L0_attn_in['wq'], 'L0_attn_wk': _L0_attn_in['wk'], 'L0_attn_wv': _L0_attn_in['wv'], 'L0_attn_wo': _L0_attn_in['wo'], 'L0_cond2_W': _L0_cond2_in['W'], 'L0_cond2_Wr': _L0_cond2_in['Wr'], 'L0_cond2_A': _L0_cond2_in['A'], 'L0_cond2_B': _L0_cond2_in['B'], 'L0_ffn_up': _L0_ffn_in['up'], 'L0_ffn_down': _L0_ffn_in['down'], 'L0_ffn_perm': _L0_ffn_in['perm']}

def reference(x, itok_B_0_30, itok_B_0_7, L0_cond_weights, L0_attn_wq, L0_attn_wk, L0_attn_wv, L0_attn_wo, L0_cond2_W, L0_cond2_Wr, L0_cond2_A, L0_cond2_B, L0_ffn_up, L0_ffn_down, L0_ffn_perm):
    import jax
    import jax.numpy as jnp

    def _L0_cond_ref(x, subjects, weights):
        import jax, jax.numpy as jnp
        import numpy as np
        B, C, D, T, S = (64, 32, 32, 512, 32)
        w = weights[subjects]
        return jnp.einsum('bct,bcd->bdt', x, w)

    def _L0_attn_ref(x, wq, wk, wv, wo):
        import math
        import jax, jax.numpy as jnp
        import numpy as np

        def _rope_tables(T, h, dtype):
            pos = jnp.arange(T, dtype=jnp.float32)
            thetas = 1.0 / 10000.0 ** (jnp.arange(0, h, 2, dtype=jnp.float32) / h)
            pt = jnp.outer(pos, thetas)
            pt = jnp.concatenate([pt, pt], axis=-1)
            return (jnp.sin(pt).astype(dtype), jnp.cos(pt).astype(dtype))

        def _apply_rope(x, sin, cos):
            h = x.shape[-1]
            rot = jnp.concatenate([-x[..., h // 2:], x[..., :h // 2]], axis=-1)
            return x * cos + rot * sin
        B, T, C = x.shape
        n_head = 32
        h = C // n_head

        def proj(w):
            y = jnp.einsum('btc,dc->btd', x, w)
            return y.reshape(B, T, n_head, h).transpose(0, 2, 1, 3)
        q, k, v = (proj(wq), proj(wk), proj(wv))
        sin, cos = _rope_tables(T, h, x.dtype)
        q = _apply_rope(q, sin, cos)
        k = _apply_rope(k, sin, cos)
        scores = jnp.einsum('bnth,bnsh->bnts', q, k) * (1.0 / math.sqrt(h))
        causal = jnp.tril(jnp.ones((T, T), dtype=bool))
        scores = jnp.where(causal, scores, -jnp.inf)
        attn = jax.nn.softmax(scores, axis=-1)
        out = jnp.einsum('bnts,bnsh->bnth', attn, v)
        out = out.transpose(0, 2, 1, 3).reshape(B, T, C)
        return jnp.einsum('btc,dc->btd', out, wo)

    def _L0_cond2_ref(x, language_ids, W, Wr, A, B):
        import jax, jax.numpy as jnp
        import numpy as np
        TOP_K = 2
        LANG_BIAS = 5.0
        SCALING = 32.0 / 16.0
        LANGUAGE_PAD_ID = -1
        base = jnp.einsum('btd,od->bto', x, W)
        E = Wr.shape[0]
        logits = jnp.einsum('btd,ed->bte', x.astype(jnp.float32), Wr.astype(jnp.float32))
        expert_targets = language_ids
        valid = expert_targets >= 0
        tgt = jnp.where(valid, expert_targets, 0)
        bias = jax.nn.one_hot(tgt, E, dtype=logits.dtype) * LANG_BIAS
        bias = jnp.where(valid[:, None], bias, 0.0)
        logits = logits + bias[:, None, :]
        topw, topi = jax.lax.top_k(logits, TOP_K)
        weights = jax.nn.softmax(topw, axis=-1)
        gates = jnp.sum(jax.nn.one_hot(topi, E, dtype=weights.dtype) * weights[..., None], axis=-2)
        gates = gates.astype(x.dtype)
        h = jnp.einsum('btd,erd->bter', x, A)
        lora_out = jnp.einsum('bter,bte,eor->bto', h, gates, B)
        return base + SCALING * lora_out

    def _L0_ffn_ref(x, up, down, perm):
        import jax, jax.numpy as jnp
        import numpy as np
        B, L, H, Dh, M = (4, 256, 16, 32, 128)
        D = H * Dh
        b, l, Dm = x.shape
        h, d = (up.shape[0], up.shape[1])
        unperm = jnp.argsort(perm)
        t = x.reshape(b * l, Dm)
        t = t[:, perm]
        t = t.reshape(b * l, h, d)
        t = jnp.einsum('bhd,hdm->bhm', t, up)
        t = jax.nn.gelu(t, approximate=False)
        t = jnp.einsum('bhm,hmd->bhd', t, down)
        t = t.reshape(b * l, h * d)
        t = t[:, unperm]
        out = t.reshape(b, l, Dm)
        return out
    x = x + _L0_attn_ref(_L0_cond_ref(x, itok_B_0_30, L0_cond_weights), L0_attn_wq, L0_attn_wk, L0_attn_wv, L0_attn_wo)
    x = x + _L0_ffn_ref(_L0_cond2_ref(x, itok_B_0_7, L0_cond2_W, L0_cond2_Wr, L0_cond2_A, L0_cond2_B), L0_ffn_up, L0_ffn_down, L0_ffn_perm)
    return x

_drawn_inputs = setup_inputs


def setup_inputs(seed=0):
    import zlib

    import numpy as np

    out = dict(_drawn_inputs(seed))
    spreads = {}
    factors = {}
    for name, (base, spread) in spreads.items():
        noise = np.random.default_rng([zlib.crc32(name.encode()), seed]).standard_normal(out[name].shape)
        drawn = base * np.exp(spread * noise) if base else spread * noise
        out[name] = jnp.asarray(drawn.astype(out[name].dtype))
    for name, factor in factors.items():
        out[name] = (out[name] * factor).astype(out[name].dtype)
    return out
```

```python
from contextlib import ExitStack

import numpy as np

import concourse.bass as bass
from concourse import mybir

F32 = mybir.dt.float32
F32R = mybir.dt.float32r
I32 = mybir.dt.int32
U32 = mybir.dt.uint32
ALU = mybir.AluOpType
ACT = mybir.ActivationFunctionType
AX_X = mybir.AxisListType.X

P = 128
B, T, D = 32, 32, 512
NH, HD = 32, 16
E, R = 8, 16
FH, FD, FM = 16, 32, 128
LANG_BIAS, SCALING = 5.0, 2.0
KC = D // P
TILES = B * T // P
BT = P // T
GT = 2
G = TILES // GT
N = GT * P
HC = P // HD
XS = 3
MASKED = -1.0e30
NEVER = -3.0e38

_AT = {}
_W = 0
for _name, _n in [("ident", P), ("cos", T), ("sin", T), ("causal", T), ("head", HC), ("seq", BT),
                  ("row", KC), ("pos", 1), ("expert", E), ("expert16", E)]:
    _AT[_name] = (_W, _W + _n)
    _W += _n
CW = _W


def constants():
    p = np.arange(P)
    c = np.zeros((P, CW), np.float32)

    def put(name, v):
        c[:, _AT[name][0]:_AT[name][1]] = v

    put("ident", np.eye(P))
    pos = np.arange(T, dtype=np.float32)
    theta = (np.float32(1.0) / np.float32(10000.0) ** (np.arange(0, HD, 2, dtype=np.float32) / np.float32(HD)))
    angle = np.outer(pos, theta.astype(np.float32)).astype(np.float32)
    by_row = angle[:, (p % HD) % (HD // 2)].T
    put("cos", np.cos(by_row))
    put("sin", np.where((p % HD < HD // 2)[:, None], -np.sin(by_row), np.sin(by_row)))
    put("causal", np.where(np.arange(T)[None] <= (p % T)[:, None], 0.0, MASKED))
    put("head", (p // HD)[:, None] == np.arange(HC)[None])
    put("seq", (p // T)[:, None] == np.arange(BT)[None])
    put("row", p[:, None] + P * np.arange(KC)[None])
    put("pos", (p % T)[:, None])
    put("expert", np.arange(E)[None])
    put("expert16", np.arange(E)[None] + 16)
    return c


def build(nc, x, subj, lang, wcond, wq, wk, wv, wo, w2, wr, wa, wb, up, down, perm, consts, cols, out):
    ctx = ExitStack()
    with ctx:
        def sb(name, shape, dt=F32):
            return ctx.enter_context(nc.sbuf_tensor(name, shape, dt))

        def sem(name):
            return ctx.enter_context(nc.semaphore(name))

        WT = {n: sb(f"{n}T", [P, 2, KC, D], F32R) for n in ("wq", "wk", "wv", "wo", "w2")}
        aT = sb("aT", [P, 2, KC, P], F32R)
        rT = sb("rT", [P, 2, KC, E], F32R)
        bT = sb("bT", [P, 2, D], F32R)
        upP = sb("upP", [P, 2, KC, 4, FM], F32R)
        dn = sb("dn", [P, FH, FD])
        unperm = sb("unperm", [P, KC, D], F32R)
        cst = sb("cst", [P, CW])

        xs = sb("xs", [P, XS, GT, D])
        wg = sb("wg", [P, TILES, T])
        wbd = sb("wbd", [P, GT, BT, T])
        xc = sb("xc", [P, 2, KC, N], F32R)
        qr = sb("qr", [P, KC, N])
        kr = sb("kr", [P, KC, N])
        rot = sb("rot", [P, 2, N])
        kbd = sb("kbd", [P, 2, BT, HC * T])
        vz = sb("vz", [P, GT, NH // 2, 3 * HD])
        pr = sb("pr", [P, 4, NH // 2, T])
        pbd = sb("pbd", [P, 2, HC, BT, T])
        x1 = sb("x1", [P, 2, KC, N], F32R)
        y2 = sb("y2", [P, 2, KC, N], F32R)
        act = sb("act", [P, 4, 2, N])
        hg = sb("hg", [P, 2, N], F32R)
        small = sb("small", [P, 280])
        idx = sb("idx", [P, TILES], U32)
        permc = sb("permc", [P, KC], I32)

        raw_q = pbd[:, :, :, :, :].rearrange("p a b c d -> p (a b c d)").rearrange("p (c k) -> p c k", c=KC)
        raw_k = act[:, :, :, :].rearrange("p a b n -> p (a b n)").rearrange("p (c k) -> p c k", c=KC)
        raw_v = pr[:, :, :, :].rearrange("p a b n -> p (a b n)").rearrange("p (c k) -> p c k", c=KC)
        raw_a = raw_q[:, 0, :]
        raw_b = raw_q[:, 1, :].rearrange("p (c e r) -> p c e r", c=KC, e=E)
        raw_r = raw_q[:, 2, :]
        raw_p = raw_q[:, 3, :].bitcast(I32)
        pick = raw_k
        kbd_flat = kbd[:, :, :, :].rearrange("p a b n -> p (a b n)")
        raw_up = kbd_flat[:, 0:D].rearrange("p (c m) -> p c m", c=KC)
        colidx = kbd_flat[:, D:2 * D]
        pT = kbd_flat.rearrange("p (i n) -> p i n", i=4)
        act_flat = act[:, :, :, :].rearrange("p a b n -> p (a b n)")
        lg = act_flat[0:E, 0:N]
        gex = act_flat[:, N:2 * N].rearrange("p (t e r) -> p t e r", t=GT, e=E)
        hs = act_flat[:, 2 * N:3 * N]
        hgf = act_flat[:, 3 * N:4 * N]

        _s = [0]

        def cut(*shape):
            n = int(np.prod(shape))
            v = small[:, _s[0]:_s[0] + n]
            _s[0] += n
            return v if len(shape) == 1 else v.rearrange("p (a b) -> p a b", a=shape[0])

        mx, sm = cut(4, NH // 2), cut(4, NH // 2)
        langf = cut(TILES)
        permf = cut(KC)
        L, eq, cand, oh1, oh2 = (cut(GT, E) for _ in range(5))
        L2 = cut(GT, E)
        m1, m2, i1, e2, g1, g2 = (cut(GT) for _ in range(6))
        ids = sb("ids", [P, 2, B], I32)

        def con(name):
            return cst[:, _AT[name][0]:_AT[name][1]]

        ident = con("ident")

        rings = {r: [ctx.enter_context(nc.psum_tensor(f"ps_{r}{i}", [P, 512], F32)) for i in range(2)]
                 for r in "ASCD"}
        full = {r: [sem(f"{r}{i}_full") for i in range(2)] for r in "ASCD"}
        free = {r: [sem(f"{r}{i}_free") for i in range(2)] for r in "ASCD"}

        def A(g, k):
            return "A", 8 * g + k

        def S_scores(g, i):
            return "S", 4 * g + 2 * max(0, g - 1) + i

        def S_down(g, h):
            return "S", 4 * min(g + 2, G) + 2 * g + h

        def C(g, k):
            return "C", 9 * g + k

        PREP = {"wq": 0, "wk": 4, "wv": 8, "a": 12, "r": 13, "b": 14, "wo": 15, "w2": 19}
        NPREP = 23

        def prep(name, k=0):
            return "D", PREP[name] + k

        def Dd(g, k):
            return "D", NPREP + 12 * g + k

        COND, Q, K_, V = 0, 2, 4, 6
        PV, WO, XT, LH, LT, GTR = 0, 2, 4, 6, 7, 8
        W_, UP, UN = 0, 2, 10

        def bank(item):
            r, n = item
            return rings[r][n % 2]

        def wait_free(eng, item):
            r, n = item
            if n >= 2:
                eng.wait_ge(free[r][n % 2], n // 2)

        def wait_full(eng, item):
            r, n = item
            eng.wait_ge(full[r][n % 2], n // 2 + 1)

        def wait_read(eng, item):
            r, n = item
            eng.wait_ge(free[r][n % 2], n // 2 + 1)

        def wait_prep(eng, name, n=4):
            for k in range(max(0, n - 2), n):
                wait_read(eng, prep(name, k))

        def wait_scored(eng, n):
            if n % 2:
                wait_full(eng, S_scores(n // 8, n // 2 % 4))
            else:
                eng.wait_ge(scored, n // 2 + 1)

        def wait_pv(eng, n):
            tile, c = n // 4, n % 4
            if c == 3:
                wait_full(eng, C(tile // GT, PV + tile % GT))
            else:
                eng.wait_ge(pv_done, 3 * tile + c + 1)

        def wait_down(eng, g, c):
            if c % 2:
                wait_full(eng, S_down(g, c // 2))
            else:
                eng.wait_ge(downed, 2 * g + c // 2 + 1)

        def s_full(item):
            return full[item[0]][item[1] % 2]

        def s_free(item):
            return free[item[0]][item[1] % 2]

        d_x = [sem(f"d_x{g}") for g in range(G)]
        d_cst, d_cols, d_ids, d_permc = sem("d_cst"), sem("d_cols"), sem("d_ids"), sem("d_permc")
        d_w = {n: sem(f"d_{n}") for n in ("wq", "wk", "wv", "wo", "w2")}
        d_lora, d_up, d_dn, d_wg = sem("d_lora"), sem("d_up"), sem("d_dn"), sem("d_wg")
        d_out = [sem(f"d_out{g}") for g in range(G)]
        idx_ready = sem("idx_ready")
        setup = sem("setup")
        wbd_ready = sem("wbd_ready")
        vz_zero = sem("vz_zero")
        prep_hi = sem("prep_hi")
        pick_ready, unperm_ready, up_hi, up_ready = sem("pick_ready"), sem("unperm_ready"), sem("up_hi"), sem("up_ready")
        xc_hi = sem("xc_hi")
        rot_shuf, rot_sin, roped = sem("rot_shuf"), sem("rot_sin"), sem("roped")
        kbd_v, kbd_p, scored = sem("kbd_v"), sem("kbd_p"), sem("scored")
        maxed, shifted, exped = sem("maxed"), sem("shifted"), sem("exped")
        summed, recip, normed, turned = sem("summed"), sem("recip"), sem("normed"), sem("turned")
        pbd_v, pbd_a, pv_done = sem("pbd_v"), sem("pbd_a"), sem("pv_done")
        o_hi = sem("o_hi")
        x1_hi = sem("x1_hi")
        h_ready, gstep, gex_ready = sem("h_ready"), sem("gstep"), sem("gex_ready")
        gap, gexp = sem("gap"), sem("gexp")
        hg_hi, hg_ready = sem("hg_hi"), sem("hg_ready")
        x2_hi = sem("x2_hi")
        downed = sem("downed")
        y_hi = sem("y_hi")

        x_d = x.rearrange("(g t b) c d -> g (b c) t d", g=G, t=GT)
        out_d = out.rearrange("(g t b) c d -> g (b c) t d", g=G, t=GT)
        w_d = {"wq": wq, "wk": wk, "wv": wv, "wo": wo}
        block = ctx.enter_context(nc.Block())

        @block.sync
        def _(sp):
            def load_x(g):
                sp.dma_start(xs[:, g % XS, :, :], x_d[g]).then_inc(d_x[g], 16)

            def load_w(name, dst):
                sp.dma_start(dst, w_d[name].rearrange("(c p) k -> p c k", p=P)).then_inc(d_w[name], 16)

            sp.dma_start(ids[:, 0, :], subj.partition_broadcast(P)).then_inc(d_ids, 16)
            sp.dma_start(ids[:, 1, :], lang.partition_broadcast(P)).then_inc(d_ids, 16)
            sp.dma_start(cst[:, :], consts).then_inc(d_cst, 16)
            load_x(0)
            load_w("wq", raw_q)
            load_w("wk", raw_k)
            sp.dma_start(colidx, cols.partition_broadcast(P)).then_inc(d_cols, 16)
            with nc.allow_non_contiguous_dma(reason="512 indices, once"):
                sp.dma_start(permc[:, :], perm.rearrange("(c p) -> p c", p=P)).then_inc(d_permc, 16)
            for j in range(4):
                sp.dma_start(raw_up[FD * j:FD * j + FD, :, :],
                             up.rearrange("(c j) d m -> j d c m", j=4)[j]).then_inc(d_up, 16)
            load_w("wv", raw_v)
            load_x(1)
            wait_prep(sp, "wq")
            sp.dma_start(raw_a, wa.rearrange("e r d -> (e r) d")).then_inc(d_lora, 16)
            for c in range(KC):
                sp.dma_start(raw_b[:, c, :, :], wb[:, P * c:P * c + P, :].rearrange("e p r -> p e r")
                             ).then_inc(d_lora, 16)
            sp.dma_start(raw_r[0:E, :], wr).then_inc(d_lora, 16)
            sp.dma_start(raw_p, perm.partition_broadcast(P)).then_inc(d_lora, 16)
            sp.dma_start(dn[:, :, :], down.rearrange("h m d -> m h d")).then_inc(d_dn, 16)
            wait_prep(sp, "b", 1)
            load_w("wo", raw_k)
            load_x(2)
            for g in range(G):
                for t in range(GT):
                    wait_read(sp, Dd(g, UN + t))
                sp.dma_start(out_d[g], xs[:, g % XS, :, :]).then_inc(d_out[g], 16)
                if g + XS < G:
                    sp.wait_ge(d_out[g], 16)
                    load_x(g + XS)
            for g in range(G):
                sp.wait_ge(d_out[g], 16)

        @block.gpsimd
        def _(pool):
            pool.memset(vz[:, :, :, :], 0.0).then_inc(vz_zero, 1)
            pool.wait_ge(idx_ready, 1)
            for t in range(TILES):
                pool.indirect_dma_start(out=wg[:, t, :], out_offset=None,
                                        in_=wcond.rearrange("s c d -> (s c) d"),
                                        in_offset=bass.IndirectOffsetOnAxis(ap=idx[:, t:t + 1], axis=0)
                                        ).then_inc(d_wg, 16)

            def rope(g, i):
                n = 4 * g + i
                dst = (qr, kr)[i // 2][:, 2 * (i % 2):2 * (i % 2) + 2, :].rearrange("p c (b d) -> p (c b) d", d=T)
                rv = rot[:, :, :].rearrange("p c (b d) -> p (c b) d", d=T)
                pool.wait_ge(rot_shuf, n + 1)
                pool.tensor_tensor(rv, rv, con("sin").unsqueeze(1).to_broadcast([P, 2 * N // T, T]),
                                   ALU.mult).then_inc(rot_sin, 1)
                pool.wait_ge(rot_sin, n + 1)
                wait_read(pool, A(g, (Q, K_)[i // 2] + i % 2))
                pool.tensor_tensor(dst, dst, rv, ALU.add).then_inc(roped, 1)

            def k_blocks(g, t, c):
                n = 8 * g + 4 * t + c
                if n == 1:
                    pool.wait_ge(up_ready, 4)
                    pool.wait_ge(unperm_ready, KC)
                pool.wait_ge(roped, 4 * g + (4 if c >= 2 else 3))
                if n >= 2:
                    wait_scored(pool, n - 2)
                if g and t == 0:
                    pool.wait_ge(pbd_v, 8 * g)
                    pool.wait_ge(pbd_a, 8 * g)
                kv = kr[:, c, P * t:P * t + P].rearrange("p (b s) -> p b s", b=BT)
                pool.tensor_tensor(
                    kbd[:, c % 2, :, :].rearrange("p b (h s) -> p b h s", h=HC),
                    kv.unsqueeze(2).to_broadcast([P, BT, HC, T]),
                    con("head").unsqueeze(1).unsqueeze(3).to_broadcast([P, BT, HC, T]),
                    ALU.mult).then_inc(kbd_p, 1)

            def shift(g, i):
                n = 4 * g + i
                pool.wait_ge(maxed, n + 1)
                pool.tensor_tensor(pr[:, i, :, :], pr[:, i, :, :],
                                   mx[:, i, :].unsqueeze(2).to_broadcast([P, NH // 2, T]),
                                   ALU.subtract).then_inc(shifted, 1)

            def norm(g, i):
                n = 4 * g + i
                pool.wait_ge(recip, n + 1)
                pool.tensor_tensor(pr[:, i, :, :], pr[:, i, :, :],
                                   mx[:, i, :].unsqueeze(2).to_broadcast([P, NH // 2, T]),
                                   ALU.mult).then_inc(normed, 1)

            for i in range(4):
                rope(0, i)
            for g in range(G):
                k_blocks(g, 0, 1)
                k_blocks(g, 0, 3)
                shift(g, 0)
                k_blocks(g, 1, 1)
                shift(g, 1)
                k_blocks(g, 1, 3)
                shift(g, 2)
                shift(g, 3)
                for i in range(4):
                    norm(g, i)
                    if g == 0:
                        rope(g + 1, i)
                if 0 < g < G - 1:
                    for i in range(4):
                        rope(g + 1, i)
                if g == 0:
                    pool.wait_ge(d_permc, 16)
                    wait_prep(pool, "wo")
                    for c in range(KC):
                        pool.indirect_dma_start(out=raw_k[:, c, :], out_offset=None, in_=w2,
                                                in_offset=bass.IndirectOffsetOnAxis(
                                                    ap=permc[:, c:c + 1].bitcast(U32), axis=0)
                                                ).then_inc(d_w["w2"], 16)

        @block.tensor
        def _(pe):
            def mm3(dst, hi_l, lo_l, hi_r, lo_r, start, stop, skip=False):
                pe.matmul(dst, hi_l, hi_r, start=start, stop=False, skip_group_check=skip)
                pe.matmul(dst, hi_l, lo_r, start=False, stop=False, skip_group_check=skip)
                return pe.matmul(dst, lo_l, hi_r, start=False, stop=stop, skip_group_check=skip)

            def prep_w(name, raw):
                pe.wait_ge(d_w[name], 64 if name == "w2" else 16)
                if name == "wq":
                    pe.wait_ge(d_cst, 16)
                for k in range(KC):
                    it = prep(name, k)
                    wait_free(pe, it)
                    for c in range(KC):
                        last = pe.transpose(bank(it)[:, P * c:P * c + P], raw[:, c, P * k:P * k + P], ident)
                    last.then_inc(s_full(it), 1)

            def cond(g):
                pe.wait_ge(d_x[g], 16)
                pe.wait_ge(wbd_ready, g + 1)
                for t in range(GT):
                    it = A(g, COND + t)
                    wait_free(pe, it)
                    for c in range(KC):
                        last = pe.matmul(bank(it)[:, P * c:P * c + P], xs[:, g % XS, t, P * c:P * c + P],
                                         wbd[:, t, :, :], start=True, stop=True)
                    last.then_inc(s_full(it), 1)

            def qk(g, name, first):
                W = WT[name]
                if name == "wq":
                    for t in range(GT):
                        wait_read(pe, A(g, COND + t))
                for i in range(2):
                    it = A(g, first + i)
                    wait_free(pe, it)
                    for h in range(2):
                        c = 2 * i + h
                        for k in range(KC):
                            last = mm3(bank(it)[:, N * h:N * h + N],
                                       W[:, 0, k, P * c:P * c + P], W[:, 1, k, P * c:P * c + P],
                                       xc[:, 0, k, :], xc[:, 1, k, :], k == 0, k == KC - 1)
                    last.then_inc(s_full(it), 1)

            def v(g, t):
                it = A(g, V + t)
                wait_free(pe, it)
                W = WT["wv"]
                for k in range(KC):
                    last = mm3(bank(it)[:, :], xc[:, 0, k, P * t:P * t + P], xc[:, 1, k, P * t:P * t + P],
                               W[:, 0, k, :], W[:, 1, k, :], k == 0, k == KC - 1)
                last.then_inc(s_full(it), 1)

            def scores(g, i):
                t, half = i // 2, i % 2
                it = S_scores(g, i)
                wait_free(pe, it)
                pe.wait_ge(roped, 4 * g + 4)
                for c in (2 * half, 2 * half + 1):
                    n = 8 * g + 4 * t + c
                    pe.wait_ge((kbd_v, kbd_p)[c % 2], n // 2 + 1)
                    for b in range(BT):
                        at = P * t + T * b
                        last = pe.matmul(bank(it)[T * b:T * b + T, N * (c % 2):N * (c % 2) + N],
                                         qr[:, c, at:at + T], kbd[:, c % 2, b, :], start=True, stop=True)
                    last.then_inc(scored if c % 2 == 0 else s_full(it), 1)

            def pv(g, t):
                it = C(g, PV + t)
                wait_free(pe, it)
                if t == 0:
                    for u in range(GT):
                        wait_read(pe, A(g, V + u))
                for c in range(KC):
                    n = 8 * g + 4 * t + c
                    pe.wait_ge(pbd_v, n + 1)
                    pe.wait_ge(pbd_a, n + 1)
                    for e in range(2):
                        for j in range(4):
                            last = pe.matmul(bank(it)[32 * j:32 * j + 32, P * c:P * c + P],
                                             vz[:, t, 4 * c + j, HD * e:HD * e + 2 * HD],
                                             pbd[:, c % 2, 2 * j + e, :, :],
                                             start=(e == 0), stop=(e == 1), skip_group_check=True)
                    last.then_inc(pv_done if c < KC - 1 else s_full(it), 1)

            def wo_proj(g, t):
                it = C(g, WO + t)
                wait_free(pe, it)
                wait_read(pe, C(g, PV + t))
                W = WT["wo"]
                for k in range(KC):
                    last = mm3(bank(it)[:, :], y2[:, 0, k, P * t:P * t + P], y2[:, 1, k, P * t:P * t + P],
                               W[:, 0, k, :], W[:, 1, k, :], k == 0, k == KC - 1)
                last.then_inc(s_full(it), 1)

            def turn_x1(g, t):
                it = C(g, XT + t)
                wait_free(pe, it)
                wait_read(pe, C(g, WO + t))
                for c in range(KC):
                    last = pe.transpose(bank(it)[:, P * c:P * c + P], xs[:, g % XS, t, P * c:P * c + P], ident)
                last.then_inc(s_full(it), 1)

            def lora_down(g):
                it = C(g, LH)
                wait_free(pe, it)
                for t in range(GT):
                    wait_read(pe, C(g, XT + t))
                for k in range(KC):
                    mm3(bank(it)[:, 0:N], aT[:, 0, k, :], aT[:, 1, k, :], x1[:, 0, k, :], x1[:, 1, k, :],
                        k == 0, k == KC - 1)
                for k in range(KC):
                    last = mm3(bank(it)[0:E, N:2 * N], rT[:, 0, k, :], rT[:, 1, k, :],
                               x1[:, 0, k, :], x1[:, 1, k, :], k == 0, k == KC - 1)
                last.then_inc(s_full(it), 1)

            def turn_logits(g):
                it = C(g, LT)
                wait_free(pe, it)
                wait_read(pe, C(g, LH))
                for t in range(GT):
                    last = pe.transpose(bank(it)[:, E * t:E * t + E], lg[:, P * t:P * t + P], ident[0:E, 0:E])
                last.then_inc(s_full(it), 1)

            def turn_gates(g):
                it = C(g, GTR)
                wait_free(pe, it)
                pe.wait_ge(gex_ready, g + 1)
                for t in range(GT):
                    last = pe.transpose(bank(it)[:, P * t:P * t + P],
                                        gex[:, t, :, :].rearrange("p e r -> p (e r)"), ident)
                last.then_inc(s_full(it), 1)

            def experts(g, i):
                it = Dd(g, W_ + i)
                wait_free(pe, it)
                W = WT["w2"]
                for h in range(2):
                    c = 2 * i + h
                    dst = bank(it)[:, N * h:N * h + N]
                    for k in range(KC):
                        mm3(dst, W[:, 0, k, P * c:P * c + P], W[:, 1, k, P * c:P * c + P],
                            x1[:, 0, k, :], x1[:, 1, k, :], k == 0, False)
                    if c == 0:
                        pe.wait_ge(hg_ready, g + 1)
                    last = mm3(dst, bT[:, 0, P * c:P * c + P], bT[:, 1, P * c:P * c + P],
                               hg[:, 0, :], hg[:, 1, :], False, True)
                last.then_inc(s_full(it), 1)

            def ffn_up(g, i):
                it = Dd(g, UP + i)
                wait_free(pe, it)
                wait_read(pe, Dd(g, W_ + i // 4))
                c = i // 2
                for h in range(2):
                    j = 2 * (i % 2) + h
                    last = mm3(bank(it)[:, N * h:N * h + N], upP[:, 0, c, j, :], upP[:, 1, c, j, :],
                               y2[:, 0, c, :], y2[:, 1, c, :], True, True)
                last.then_inc(s_full(it), 1)

            def ffn_down(g, c):
                it = S_down(g, c // 2)
                if c % 2 == 0:
                    wait_free(pe, it)
                for i in range(2):
                    wait_read(pe, Dd(g, UP + 2 * c + i))
                for j in range(4):
                    last = pe.matmul(bank(it)[32 * j:32 * j + 32, N * (c % 2):N * (c % 2) + N],
                                     dn[:, 4 * c + j, :], act[:, (2 * c + j // 2) % 4, j % 2, :],
                                     start=True, stop=True)
                last.then_inc(downed if c % 2 == 0 else s_full(it), 1)

            def unpermute(g, t):
                it = Dd(g, UN + t)
                wait_free(pe, it)
                for i in range(2):
                    wait_read(pe, S_down(g, i))
                for c in range(KC):
                    for part in range(2):
                        last = pe.matmul(bank(it)[:, :], y2[:, part, c, P * t:P * t + P], unperm[:, c, :],
                                         start=(c == 0 and part == 0), stop=(c == KC - 1 and part == 1))
                last.then_inc(s_full(it), 1)

            def ffn(g):
                turn_gates(g)
                experts(g, 0)
                experts(g, 1)
                for i in range(4):
                    ffn_up(g, i)
                ffn_down(g, 0)
                ffn_up(g, 4)
                ffn_up(g, 5)
                ffn_down(g, 1)
                ffn_up(g, 6)
                ffn_up(g, 7)
                ffn_down(g, 2)
                ffn_down(g, 3)
                unpermute(g, 0)
                unpermute(g, 1)

            cond(0)
            prep_w("wq", raw_q)
            wait_prep(pe, "wq")
            qk(0, "wq", Q)
            prep_w("wk", raw_k)
            wait_prep(pe, "wk")
            qk(0, "wk", K_)
            prep_w("wv", raw_v)
            wait_prep(pe, "wv")
            v(0, 0)
            v(0, 1)
            pe.wait_ge(d_lora, 16 * (3 + KC))
            it = prep("a")
            wait_free(pe, it)
            for k in range(KC):
                last = pe.transpose(bank(it)[:, P * k:P * k + P], raw_a[:, P * k:P * k + P], ident)
            last.then_inc(s_full(it), 1)
            it = prep("r")
            wait_free(pe, it)
            for k in range(KC):
                last = pe.transpose(bank(it)[:, E * k:E * k + E], raw_r[0:E, P * k:P * k + P], ident[0:E, 0:E])
            last.then_inc(s_full(it), 1)
            it = prep("b")
            wait_free(pe, it)
            pe.wait_ge(pick_ready, KC)
            for c in range(KC):
                last = pe.matmul(bank(it)[:, :], raw_b[:, c, :, :].rearrange("p e r -> p (e r)"), pick[:, c, :],
                                 start=(c == 0), stop=(c == KC - 1))
            last.then_inc(s_full(it), 1)
            for g in range(G):
                if g + 1 < G:
                    cond(g + 1)
                if g:
                    lora_down(g - 1)
                scores(g, 0)
                scores(g, 1)
                if g:
                    turn_logits(g - 1)
                scores(g, 2)
                scores(g, 3)
                if g == 0:
                    prep_w("wo", raw_k)
                else:
                    ffn(g - 1)
                if g + 1 < G:
                    qk(g + 1, "wq", Q)
                    qk(g + 1, "wk", K_)
                pv(g, 0)
                pv(g, 1)
                if g + 1 < G:
                    v(g + 1, 0)
                if g == 0:
                    wait_prep(pe, "wo")
                wo_proj(g, 0)
                if g + 1 < G:
                    v(g + 1, 1)
                wo_proj(g, 1)
                turn_x1(g, 0)
                turn_x1(g, 1)
                if g == 0:
                    prep_w("w2", raw_k)
                    for name, n in (("a", 1), ("r", 1), ("b", 1), ("w2", 4)):
                        wait_prep(pe, name, n)
                    pe.wait_ge(up_ready, 4)
                    pe.wait_ge(unperm_ready, KC)
                    pe.wait_ge(d_dn, 16)
            lora_down(G - 1)
            turn_logits(G - 1)
            ffn(G - 1)

        @block.scalar
        def _(sc):
            def copy(dst, src):
                return sc.activation(dst, src, ACT.Copy)

            def prep_his(name, n, dst):
                for k in range(n):
                    it = prep(name, k)
                    wait_full(sc, it)
                    copy(dst(k), bank(it)[:, 0:dst(k).free_size()]).then_inc(prep_hi, 1)

            def cond_hi(g, t):
                it = A(g, COND + t)
                wait_full(sc, it)
                copy(xc[:, 0, :, P * t:P * t + P], bank(it)[:, :].rearrange("p (c n) -> p c n", c=KC)
                     ).then_inc(xc_hi, 1)

            def v_out(g, t):
                it = A(g, V + t)
                if g == 0 and t == 0:
                    sc.wait_ge(vz_zero, 1)
                wait_full(sc, it)
                dst = vz[:, t, :, :].rearrange("p q (s f) -> p q s f", f=HD)[:, :, 0:3:2, :]
                copy(dst, bank(it)[:, :].rearrange("p (q s f) -> p q s f", s=2, f=HD)).then_inc(s_free(it), 1)

            def exp(g, i):
                sc.wait_ge(shifted, 4 * g + i + 1)
                sc.activation(pr[:, i, :, :], pr[:, i, :, :], ACT.Exp, scale=float(HD) ** -0.5
                              ).then_inc(exped, 1)

            def gate_exp(g):
                sc.wait_ge(gap, g + 1)
                sc.activation(e2, e2, ACT.Exp).then_inc(gexp, 1)

            def h_out(g):
                it = C(g, LH)
                wait_full(sc, it)
                copy(hs, bank(it)[:, 0:N]).then_inc(h_ready, 1)

            def probs_block(g, t, c):
                n = 8 * g + 4 * t + c
                sc.wait_ge(turned, 4 * g + 2 * t + c // 2 + 1)
                if n >= 2:
                    wait_pv(sc, n - 2)
                if n == 0:
                    wait_prep(sc, "b", 1)
                src = pT[:, 2 * t + c // 2, N * (c % 2):N * (c % 2) + N].rearrange("p (h s) -> p h s", h=HC)
                b = BT - 1
                sc.activation(pbd[:, c % 2, :, b, :], src, ACT.Copy, scale=con("seq")[:, b:b + 1]
                              ).then_inc(pbd_a, 1)

            def split_hi(it, dst, s):
                wait_full(sc, it)
                copy(dst, bank(it)[:, :].rearrange("p (c n) -> p c n", n=dst.shape[-1])).then_inc(s, 1)

            def gelu(g, i):
                it = Dd(g, UP + i)
                n = 8 * g + i
                wait_full(sc, it)
                if n >= 4:
                    wait_down(sc, (n - 4) // 8, (n - 4) % 8 // 2)
                sc.activation(act[:, i % 4, :, :], bank(it)[:, :].rearrange("p (h n) -> p h n", h=2), ACT.Gelu
                              ).then_inc(s_free(it), 1)

            def ffn(g):
                for i in range(2):
                    split_hi(Dd(g, W_ + i), y2[:, 0, 2 * i:2 * i + 2, :], x2_hi)
                for i in range(6):
                    gelu(g, i)
                split_hi(S_down(g, 0), y2[:, 0, 0:2, :], y_hi)
                gelu(g, 6)
                gelu(g, 7)
                split_hi(S_down(g, 1), y2[:, 0, 2:4, :], y_hi)

            cond_hi(0, 0)
            cond_hi(0, 1)
            prep_his("wq", KC, lambda k: WT["wq"][:, 0, k, :])
            prep_his("wk", KC, lambda k: WT["wk"][:, 0, k, :])
            prep_his("wv", KC, lambda k: WT["wv"][:, 0, k, :])
            v_out(0, 0)
            v_out(0, 1)
            prep_his("a", 1, lambda k: aT[:, 0, :, :].rearrange("p a b -> p (a b)"))
            prep_his("r", 1, lambda k: rT[:, 0, :, :].rearrange("p a b -> p (a b)"))
            prep_his("b", 1, lambda k: bT[:, 0, :])
            for g in range(G):
                if g + 1 < G:
                    cond_hi(g + 1, 0)
                    cond_hi(g + 1, 1)
                if g:
                    h_out(g - 1)
                exp(g, 0)
                exp(g, 1)
                if g:
                    gate_exp(g - 1)
                exp(g, 2)
                exp(g, 3)
                if g == 0:
                    prep_his("wo", KC, lambda k: WT["wo"][:, 0, k, :])
                else:
                    ffn(g - 1)
                for c in range(KC):
                    probs_block(g, 0, c)
                probs_block(g, 1, 0)
                probs_block(g, 1, 1)
                split_hi(C(g, PV), y2[:, 0, :, 0:P], o_hi)
                probs_block(g, 1, 2)
                probs_block(g, 1, 3)
                split_hi(C(g, PV + 1), y2[:, 0, :, P:2 * P], o_hi)
                if g + 1 < G:
                    v_out(g + 1, 0)
                    v_out(g + 1, 1)
                for t in range(GT):
                    split_hi(C(g, XT + t), x1[:, 0, :, P * t:P * t + P], x1_hi)
                if g == 0:
                    prep_his("w2", KC, lambda k: WT["w2"][:, 0, k, :])
            h_out(G - 1)
            gate_exp(G - 1)
            ffn(G - 1)

        @block.vector
        def _(ve):
            steps = [0]

            def step(ins):
                steps[0] += 1
                ins.then_inc(setup, 1)
                ve.wait_ge(setup, steps[0])

            def split_lo(it, hi, lo, s_hi, n_hi):
                ve.wait_ge(s_hi, n_hi)
                src = bank(it)[:, 0:hi.free_size()]
                if len(hi.shape) == 3:
                    src = src.rearrange("p (c n) -> p c n", n=hi.shape[-1])
                wait_full(ve, it)
                ve.tensor_tensor(lo, src, hi.bitcast(F32), ALU.subtract).then_inc(s_free(it), 1)

            def prep_los(name, n, w):
                for k in range(n):
                    it = prep(name, k)
                    split_lo(it, w(k, 0), w(k, 1), prep_hi, it[1] + 1)

            def cond_lo(g, t):
                at = slice(P * t, P * t + P)
                split_lo(A(g, COND + t), xc[:, 0, :, at], xc[:, 1, :, at], xc_hi, GT * g + t + 1)

            def blocks(g):
                if g:
                    wait_full(ve, A(g - 1, COND + 1))
                for b in range(BT):
                    i = ve.tensor_scalar(wbd[:, :, b, :], wg[:, GT * g:GT * g + GT, :],
                                         con("seq")[:, b:b + 1], None, ALU.mult)
                i.then_inc(wbd_ready, 1)

            def rope(g, i):
                n = 4 * g + i
                it = A(g, (Q, K_)[i // 2] + i % 2)
                dst = (qr, kr)[i // 2][:, 2 * (i % 2):2 * (i % 2) + 2, :].rearrange("p c (b d) -> p (c b) d", d=T)
                src = bank(it)[:, :]
                wait_full(ve, it)
                if n:
                    ve.wait_ge(roped, n)
                half = HD // 2
                order = [(j + half) if j % HD < half else (j - half) for j in range(32)]
                ve.stream_shuffle(rot[:, :, :].rearrange("p c n -> p (c n)"), src, order).then_inc(rot_shuf, 1)
                ve.tensor_tensor(dst, src.rearrange("p (c d) -> p c d", d=T),
                                 con("cos").unsqueeze(1).to_broadcast([P, 2 * N // T, T]), ALU.mult
                                 ).then_inc(s_free(it), 1)

            def k_blocks(g, t, c):
                n = 8 * g + 4 * t + c
                ve.wait_ge(roped, 4 * g + (4 if c >= 2 else 3))
                if n >= 2:
                    wait_scored(ve, n - 2)
                if n == 0:
                    ve.wait_ge(unperm_ready, KC)
                if g and t == 0:
                    ve.wait_ge(pbd_a, 8 * g)
                kv = kr[:, c, P * t:P * t + P].rearrange("p (b s) -> p b s", b=BT)
                ve.tensor_tensor(
                    kbd[:, c % 2, :, :].rearrange("p b (h s) -> p b h s", h=HC),
                    kv.unsqueeze(2).to_broadcast([P, BT, HC, T]),
                    con("head").unsqueeze(1).unsqueeze(3).to_broadcast([P, BT, HC, T]),
                    ALU.mult).then_inc(kbd_v, 1)

            def mask_max(g, i):
                it = S_scores(g, i)
                n = 4 * g + i
                wait_full(ve, it)
                if n == 0:
                    wait_prep(ve, "wv")
                ve.tensor_tensor(pr[:, i, :, :], bank(it)[:, :].rearrange("p (h s) -> p h s", s=T),
                                 con("causal").unsqueeze(1).to_broadcast([P, NH // 2, T]), ALU.add
                                 ).then_inc(s_free(it), 1)
                wait_read(ve, it)
                ve.tensor_reduce(mx[:, i, :], pr[:, i, :, :], AX_X, ALU.max).then_inc(maxed, 1)

            def sums(g, i):
                n = 4 * g + i
                ve.wait_ge(exped, n + 1)
                ve.tensor_reduce(sm[:, i, :], pr[:, i, :, :], AX_X, ALU.add).then_inc(summed, 1)
                ve.wait_ge(summed, n + 1)
                ve.reciprocal(mx[:, i, :], sm[:, i, :]).then_inc(recip, 1)

            def turn(g, i):
                ve.wait_ge(normed, 4 * g + i + 1)
                ve.transpose(pT[:, i, :], pr[:, i, :, :].rearrange("p h s -> p (h s)")).then_inc(turned, 1)

            def probs_blocks(g, t, c):
                n = 8 * g + 4 * t + c
                ve.wait_ge(turned, 4 * g + 2 * t + c // 2 + 1)
                if n >= 2:
                    wait_pv(ve, n - 2)
                if n == 0:
                    wait_prep(ve, "b", 1)
                src = pT[:, 2 * t + c // 2, N * (c % 2):N * (c % 2) + N].rearrange("p (h s) -> p h s", h=HC)
                for b in range(BT - 1):
                    i = ve.tensor_scalar(pbd[:, c % 2, :, b, :], src, con("seq")[:, b:b + 1], None, ALU.mult)
                i.then_inc(pbd_v, 1)

            def o_lo(g, t):
                at = slice(P * t, P * t + P)
                split_lo(C(g, PV + t), y2[:, 0, :, at], y2[:, 1, :, at], o_hi, GT * g + t + 1)

            def add_x(g, t):
                it = C(g, WO + t)
                wait_full(ve, it)
                ve.tensor_tensor(xs[:, g % XS, t, :], bank(it)[:, :], xs[:, g % XS, t, :], ALU.add
                                 ).then_inc(s_free(it), 1)

            def x1_lo(g, t):
                at = slice(P * t, P * t + P)
                split_lo(C(g, XT + t), x1[:, 0, :, at], x1[:, 1, :, at], x1_hi, GT * g + t + 1)

            def logits_out(g):
                it = C(g, LH)
                wait_full(ve, it)
                ve.wait_ge(h_ready, g + 1)
                ve.tensor_copy(lg, bank(it)[0:E, N:2 * N]).then_inc(s_free(it), 1)

            gsteps = [0]

            def gate(ins):
                gsteps[0] += 1
                ins.then_inc(gstep, 1)
                ve.wait_ge(gstep, gsteps[0])

            def gates(g):
                it = C(g, LT)
                wide = [P, GT, E]

                def w(v):
                    return v.unsqueeze(2).to_broadcast(wide)

                experts_, experts16 = (con(n).unsqueeze(1).to_broadcast(wide) for n in ("expert", "expert16"))
                gate(ve.tensor_tensor(eq, experts_, w(langf[:, GT * g:GT * g + GT]), ALU.is_equal))
                wait_full(ve, it)
                ve.scalar_tensor_tensor(out=L, in0=eq, scalar=LANG_BIAS,
                                        in1=bank(it)[:, 0:GT * E].rearrange("p (t e) -> p t e", t=GT),
                                        op0=ALU.mult, op1=ALU.add).then_inc(s_free(it), 1)
                wait_read(ve, it)
                for src, m, oh in ((L, m1, oh1), (L2, m2, oh2)):
                    gate(ve.tensor_reduce(m, src, AX_X, ALU.max))
                    gate(ve.tensor_tensor(eq, src, w(m), ALU.is_equal))
                    gate(ve.scalar_tensor_tensor(out=cand, in0=eq, scalar=-16.0, in1=experts16,
                                                 op0=ALU.mult, op1=ALU.add))
                    gate(ve.tensor_reduce(i1, cand, AX_X, ALU.min))
                    gate(ve.tensor_tensor(oh, experts_, w(i1), ALU.is_equal))
                    if oh is oh1:
                        gate(ve.scalar_tensor_tensor(out=L2, in0=oh1, scalar=NEVER, in1=L,
                                                     op0=ALU.mult, op1=ALU.add))
                ve.tensor_tensor(e2, m2, m1, ALU.subtract).then_inc(gap, 1)
                ve.wait_ge(gexp, g + 1)
                gate(ve.tensor_scalar(g2, e2, 1.0, None, ALU.add))
                gate(ve.reciprocal(g1, g2))
                gate(ve.tensor_tensor(g2, e2, g1, ALU.mult))
                gate(ve.tensor_tensor(oh1, oh1, w(g1), ALU.mult))
                gate(ve.tensor_tensor(oh2, oh2, w(g2), ALU.mult))
                gate(ve.tensor_tensor(cand, oh1, oh2, ALU.add))
                ve.tensor_scalar(gex, cand.unsqueeze(3).to_broadcast([P, GT, E, R]), SCALING, None,
                                 ALU.mult).then_inc(gex_ready, 1)

            def gate_h(g):
                it = C(g, GTR)
                wait_full(ve, it)
                ve.wait_ge(h_ready, g + 1)
                ve.tensor_tensor(hgf, bank(it)[:, 0:N], hs, ALU.mult).then_inc(s_free(it), 1)
                wait_read(ve, it)
                ve.tensor_copy(hg[:, 0, :], hgf).then_inc(hg_hi, 1)
                ve.wait_ge(hg_hi, g + 1)
                ve.tensor_tensor(hg[:, 1, :], hgf, hg[:, 0, :].bitcast(F32), ALU.subtract).then_inc(hg_ready, 1)

            def x2_lo(g, i):
                at = slice(2 * i, 2 * i + 2)
                split_lo(Dd(g, W_ + i), y2[:, 0, at, :], y2[:, 1, at, :], x2_hi, 2 * g + i + 1)

            def y_lo(g, i):
                at = slice(2 * i, 2 * i + 2)
                split_lo(S_down(g, i), y2[:, 0, at, :], y2[:, 1, at, :], y_hi, 2 * g + i + 1)

            def add_ffn(g, t):
                it = Dd(g, UN + t)
                wait_full(ve, it)
                ve.tensor_tensor(xs[:, g % XS, t, :], bank(it)[:, :], xs[:, g % XS, t, :], ALU.add
                                 ).then_inc(s_free(it), 1)

            ve.wait_ge(d_ids, 32)
            ve.wait_ge(d_cst, 16)
            for b in range(BT):
                at = slice(T * b, T * b + T)
                i = ve.tensor_scalar(idx[at, :], ids[at, 0, b:B:BT], float(T), con("pos")[at, :],
                                     ALU.mult, ALU.add)
            i.then_inc(idx_ready, 1)
            for b in range(BT):
                at = slice(T * b, T * b + T)
                i = ve.tensor_copy(langf[at, :], ids[at, 1, b:B:BT])
            step(i)
            ve.wait_ge(d_wg, 16 * TILES)
            blocks(0)
            cond_lo(0, 0)
            cond_lo(0, 1)
            blocks(1)
            prep_los("wq", KC, lambda k, s: WT["wq"][:, s, k, :])
            rope(0, 0)
            rope(0, 1)
            ve.wait_ge(d_permc, 16)
            step(ve.tensor_copy(permf, permc[:, :]))
            ve.wait_ge(d_cols, 16)
            for c in range(KC):
                ve.tensor_scalar(unperm[:, c, :], colidx, permf[:, c:c + 1], None, ALU.is_equal
                                 ).then_inc(unperm_ready, 1)
            prep_los("wk", KC, lambda k, s: WT["wk"][:, s, k, :])
            rope(0, 2)
            rope(0, 3)
            ve.wait_ge(d_up, 64)
            for j in range(4):
                ve.tensor_scalar(upP[:, 0, :, j, :], raw_up, con("seq")[:, j:j + 1], None, ALU.mult
                                 ).then_inc(up_hi, 1)
            for j in range(4):
                ve.wait_ge(up_hi, j + 1)
                ve.scalar_tensor_tensor(out=upP[:, 1, :, j, :], in0=raw_up, scalar=con("seq")[:, j:j + 1],
                                        in1=upP[:, 0, :, j, :].bitcast(F32), op0=ALU.mult, op1=ALU.subtract
                                        ).then_inc(up_ready, 1)
            prep_los("wv", KC, lambda k, s: WT["wv"][:, s, k, :])
            ve.wait_ge(d_lora, 16 * (3 + KC))
            for c in range(KC):
                ve.tensor_scalar(pick[:, c, :], raw_p, con("row")[:, c:c + 1], None, ALU.is_equal
                                 ).then_inc(pick_ready, 1)
            prep_los("a", 1, lambda k, s: aT[:, s, :, :].rearrange("p a b -> p (a b)"))
            prep_los("r", 1, lambda k, s: rT[:, s, :, :].rearrange("p a b -> p (a b)"))
            prep_los("b", 1, lambda k, s: bT[:, s, :])
            for g in range(G):
                if g + 1 < G:
                    cond_lo(g + 1, 0)
                    cond_lo(g + 1, 1)
                    if g + 2 < G:
                        blocks(g + 2)
                if g:
                    logits_out(g - 1)
                k_blocks(g, 0, 0)
                k_blocks(g, 0, 2)
                mask_max(g, 0)
                k_blocks(g, 1, 0)
                mask_max(g, 1)
                k_blocks(g, 1, 2)
                if g:
                    gates(g - 1)
                mask_max(g, 2)
                mask_max(g, 3)
                if g == 0:
                    prep_los("wo", KC, lambda k, s: WT["wo"][:, s, k, :])
                    for i in range(4):
                        sums(g, i)
                        if i:
                            turn(g, i - 1)
                        rope(g + 1, i)
                    turn(g, 3)
                else:
                    gate_h(g - 1)
                    sums(g, 0)
                    x2_lo(g - 1, 0)
                    sums(g, 1)
                    turn(g, 0)
                    x2_lo(g - 1, 1)
                    sums(g, 2)
                    turn(g, 1)
                    sums(g, 3)
                    turn(g, 2)
                    turn(g, 3)
                    y_lo(g - 1, 0)
                    y_lo(g - 1, 1)
                    add_ffn(g - 1, 0)
                    add_ffn(g - 1, 1)
                    if g + 1 < G:
                        for i in range(4):
                            rope(g + 1, i)
                for c in range(KC):
                    probs_blocks(g, 0, c)
                probs_blocks(g, 1, 0)
                probs_blocks(g, 1, 1)
                o_lo(g, 0)
                probs_blocks(g, 1, 2)
                probs_blocks(g, 1, 3)
                o_lo(g, 1)
                add_x(g, 0)
                add_x(g, 1)
                x1_lo(g, 0)
                x1_lo(g, 1)
                if g == 0:
                    prep_los("w2", KC, lambda k, s: WT["w2"][:, s, k, :])
            logits_out(G - 1)
            gates(G - 1)
            gate_h(G - 1)
            x2_lo(G - 1, 0)
            x2_lo(G - 1, 1)
            y_lo(G - 1, 0)
            y_lo(G - 1, 1)
            add_ffn(G - 1, 0)
            add_ffn(G - 1, 1)


_INS = ["x", "itok_B_0_30", "itok_B_0_7", "L0_cond_weights", "L0_attn_wq", "L0_attn_wk", "L0_attn_wv",
        "L0_attn_wo", "L0_cond2_W", "L0_cond2_Wr", "L0_cond2_A", "L0_cond2_B", "L0_ffn_up", "L0_ffn_down",
        "L0_ffn_perm"]


def kernel(**inputs):
    import concourse.bacc as _bacc
    from concourse.bass_utils import run_bass_kernel_spmd as _run

    nc = _bacc.Bacc("TRN2", target_bir_lowering=False, num_devices=1)
    arrays, args = {}, []

    def give(name, a):
        a = np.ascontiguousarray(a)
        arrays[name] = a
        args.append(nc.dram_tensor(name, a.shape, mybir.dt.from_np(a.dtype), kind="ExternalInput").ap())

    for name in _INS:
        give(f"in_{name}", inputs[name])
    give("constants", constants())
    give("columns", np.arange(D, dtype=np.float32))
    args.append(nc.dram_tensor("out_0", (B, T, D), F32, kind="ExternalOutput").ap())
    build(nc, *args)
    r = _run(nc, [arrays], core_ids=[0])
    return r.results[0]["out_0"]
```

```python
from contextlib import ExitStack

import numpy as np

import concourse.bass as bass
from concourse import mybir

F32 = mybir.dt.float32
F32R = mybir.dt.float32r
I32 = mybir.dt.int32
U32 = mybir.dt.uint32
ALU = mybir.AluOpType
ACT = mybir.ActivationFunctionType
AX_X = mybir.AxisListType.X

P = 128
B, T, D = 32, 32, 512
NH, HD = 32, 16
E, R = 8, 16
FH, FD, FM = 16, 32, 128
LANG_BIAS, SCALING = 5.0, 2.0
KC = D // P
TILES = B * T // P
BT = P // T
GT = 2
G = TILES // GT
N = GT * P
HC = P // HD
XS = 3
MASKED = -1.0e30
NEVER = -3.0e38

_AT = {}
_W = 0
for _name, _n in [("ident", P), ("cos", T), ("sin", T), ("causal", T), ("head", HC), ("seq", BT),
                  ("row", KC), ("pos", 1), ("expert", E), ("expert16", E)]:
    _AT[_name] = (_W, _W + _n)
    _W += _n
CW = _W


def constants():
    p = np.arange(P)
    c = np.zeros((P, CW), np.float32)

    def put(name, v):
        c[:, _AT[name][0]:_AT[name][1]] = v

    put("ident", np.eye(P))
    pos = np.arange(T, dtype=np.float32)
    theta = (np.float32(1.0) / np.float32(10000.0) ** (np.arange(0, HD, 2, dtype=np.float32) / np.float32(HD)))
    angle = np.outer(pos, theta.astype(np.float32)).astype(np.float32)
    by_row = angle[:, (p % HD) % (HD // 2)].T
    put("cos", np.cos(by_row))
    put("sin", np.where((p % HD < HD // 2)[:, None], -np.sin(by_row), np.sin(by_row)))
    put("causal", np.where(np.arange(T)[None] <= (p % T)[:, None], 0.0, MASKED))
    put("head", (p // HD)[:, None] == np.arange(HC)[None])
    put("seq", (p // T)[:, None] == np.arange(BT)[None])
    put("row", p[:, None] + P * np.arange(KC)[None])
    put("pos", (p % T)[:, None])
    put("expert", np.arange(E)[None])
    put("expert16", np.arange(E)[None] + 16)
    return c


def build(nc, x, subj, lang, wcond, wq, wk, wv, wo, w2, wr, wa, wb, up, down, perm, consts, cols, out):
    ctx = ExitStack()
    with ctx:
        def sb(name, shape, dt=F32):
            return ctx.enter_context(nc.sbuf_tensor(name, shape, dt))

        def sem(name):
            return ctx.enter_context(nc.semaphore(name))

        WT = {n: sb(f"{n}T", [P, 2, KC, D], F32R) for n in ("wq", "wk", "wv", "wo", "w2")}
        aT = sb("aT", [P, 2, KC, P], F32R)
        rT = sb("rT", [P, 2, KC, E], F32R)
        bT = sb("bT", [P, 2, D], F32R)
        upP = sb("upP", [P, 2, KC, 4, FM], F32R)
        dn = sb("dn", [P, FH, FD])
        unperm = sb("unperm", [P, KC, D], F32R)
        cst = sb("cst", [P, CW])

        xs = sb("xs", [P, XS, GT, D])
        wg = sb("wg", [P, TILES, T])
        wbd = sb("wbd", [P, GT, BT, T])
        xc = sb("xc", [P, 2, KC, N], F32R)
        qr = sb("qr", [P, KC, N])
        kr = sb("kr", [P, KC, N])
        rot = sb("rot", [P, 2, N])
        kbd = sb("kbd", [P, KC, BT, HC * T])
        vz = sb("vz", [P, GT, NH // 2, 3 * HD])
        pr = sb("pr", [P, 5, NH // 2, T])
        pbd = sb("pbd", [P, 2, HC, BT, T])
        x1 = sb("x1", [P, 2, KC, N], F32R)
        y2 = sb("y2", [P, 2, KC, N], F32R)
        act = sb("act", [P, 4, 2, N])
        hg = sb("hg", [P, 2, N], F32R)
        small = sb("small", [P, 348])
        idx = sb("idx", [P, TILES], U32)
        permc = sb("permc", [P, KC], I32)

        raw_q = pbd[:, :, :, :, :].rearrange("p a b c d -> p (a b c d)").rearrange("p (c k) -> p c k", c=KC)
        raw_k = act[:, :, :, :].rearrange("p a b n -> p (a b n)").rearrange("p (c k) -> p c k", c=KC)
        raw_v = pr[:, 0:4, :, :].rearrange("p a b n -> p (a b n)").rearrange("p (c k) -> p c k", c=KC)
        raw_a = raw_q[:, 0, :]
        raw_b = raw_q[:, 1, :].rearrange("p (c e r) -> p c e r", c=KC, e=E)
        raw_r = raw_q[:, 2, :]
        raw_p = raw_q[:, 3, :].bitcast(I32)
        pick = raw_v
        raw_o = xs[:, 1:3, :, :].rearrange("p a t d -> p (a t) d")
        raw_w2 = raw_k
        kbd_flat = kbd[:, :, :, :].rearrange("p a b n -> p (a b n)")
        raw_up = kbd_flat[:, 0:D].rearrange("p (c m) -> p c m", c=KC)
        colidx = pr[:, 4, :, :].rearrange("p h s -> p (h s)")

        def pT(i):
            return pr[:, (i - 1) % 5, :, :]

        act_flat = act[:, :, :, :].rearrange("p a b n -> p (a b n)")
        lg = act_flat[0:E, 0:N]
        gex = act_flat[:, N:2 * N].rearrange("p (t e r) -> p t e r", t=GT, e=E)
        hs = act_flat[:, 2 * N:3 * N]
        hgf = act_flat[:, 3 * N:4 * N]

        _s = [0]

        def cut(*shape):
            n = int(np.prod(shape))
            v = small[:, _s[0]:_s[0] + n]
            _s[0] += n
            return v if len(shape) == 1 else v.rearrange("p (a b) -> p a b", a=shape[0])

        mx, sm = cut(4, NH // 2), cut(4, NH // 2)
        langf = cut(TILES)
        bias = cut(TILES, E)
        permf = cut(KC)
        unused = cut(G)
        L, eq, cand, oh1, oh2 = (cut(GT, E) for _ in range(5))
        L2 = cut(GT, E)
        m1, m2, i1, e2, g1, g2 = (cut(GT) for _ in range(6))
        ids = sb("ids", [P, 2, B], I32)

        def con(name):
            return cst[:, _AT[name][0]:_AT[name][1]]

        ident = con("ident")

        rings = {r: [ctx.enter_context(nc.psum_tensor(f"ps_{r}{i}", [P, 512], F32)) for i in range(2)]
                 for r in "ASCD"}
        full = {r: [sem(f"{r}{i}_full") for i in range(2)] for r in "ASCD"}
        free = {r: [sem(f"{r}{i}_free") for i in range(2)] for r in "ASCD"}

        def A(g, k):
            return "A", 8 * g + k

        def S_scores(g, i):
            return "S", 4 * g + 2 * max(0, g - 1) + i

        def S_down(g, h):
            return "S", 4 * min(g + 2, G) + 2 * g + h

        def C(g, k):
            return "C", NPREP - D_PREP + 9 * g + k

        PREP = {"wq": 0, "wk": 4, "wv": 8, "w2": 12, "wo": 16, "b": 20, "a": 21, "r": 22}
        NPREP = 23

        def prep(name, k=0):
            n = PREP[name] + k
            return "DC"[n // 2 % 2], n // 4 * 2 + n % 2

        D_PREP = sum(n // 2 % 2 == 0 for n in range(NPREP))

        def Dd(g, k):
            return "D", D_PREP + 12 * g + k

        COND, Q, K_, V = 0, 2, 4, 6
        PV, WO, XT, LH, LT, GTR = 0, 2, 4, 6, 7, 8
        W_, UP, UN = 0, 2, 10

        def bank(item):
            r, n = item
            return rings[r][n % 2]

        def wait_free(eng, item):
            r, n = item
            if n >= 2:
                eng.wait_ge(free[r][n % 2], n // 2)

        def wait_full(eng, item):
            r, n = item
            eng.wait_ge(full[r][n % 2], n // 2 + 1)

        def wait_read(eng, item):
            r, n = item
            eng.wait_ge(free[r][n % 2], n // 2 + 1)

        def wait_prep(eng, name, n=4):
            wait_read(eng, prep(name, n - 1))

        def wait_scored(eng, n):
            if n % 2:
                wait_full(eng, S_scores(n // 8, n // 2 % 4))
            else:
                eng.wait_ge(scored, n // 2 + 1)

        def wait_pv(eng, n):
            tile, c = n // 4, n % 4
            if c == 3:
                wait_full(eng, C(tile // GT, PV + tile % GT))
            else:
                eng.wait_ge(pv_done, 3 * tile + c + 1)

        def wait_down(eng, g, c):
            if c % 2:
                wait_full(eng, S_down(g, c // 2))
            else:
                eng.wait_ge(downed, 2 * g + c // 2 + 1)

        def s_full(item):
            return full[item[0]][item[1] % 2]

        def s_free(item):
            return free[item[0]][item[1] % 2]

        d_x = [sem(f"d_x{g}") for g in range(G)]
        d_cst, d_cols, d_ids, d_permc = sem("d_cst"), sem("d_cols"), sem("d_ids"), sem("d_permc")
        d_w = {n: sem(f"d_{n}") for n in ("wq", "wk", "wv", "wo", "w2")}
        d_lora, d_up, d_dn, d_wg = sem("d_lora"), sem("d_up"), sem("d_dn"), [sem(f"d_wg{g}") for g in range(G)]
        d_out = [sem(f"d_out{g}") for g in range(G)]
        idx_ready, permf_ready = sem("idx_ready"), sem("permf_ready")
        setup = sem("setup")
        wbd_ready = sem("wbd_ready")
        vz_zero = sem("vz_zero")
        prep_hi = sem("prep_hi")
        pick_ready, unperm_ready, up_hi, up_ready = sem("pick_ready"), sem("unperm_ready"), sem("up_hi"), sem("up_ready")
        xc_hi = sem("xc_hi")
        rot_shuf, rot_sin, roped = sem("rot_shuf"), sem("rot_sin"), sem("roped")
        kbd_v, kbd_p, scored = sem("kbd_v"), sem("kbd_p"), sem("scored")
        maxed, shifted, exped = sem("maxed"), sem("shifted"), sem("exped")
        summed, recip, normed, turned = sem("summed"), sem("recip"), sem("normed"), sem("turned")
        pbd_v, pbd_a, pv_done = sem("pbd_v"), sem("pbd_a"), sem("pv_done")
        o_hi = sem("o_hi")
        x1_hi = sem("x1_hi")
        h_ready, gstep, gex_ready = sem("h_ready"), sem("gstep"), sem("gex_ready")
        gap, gexp = sem("gap"), sem("gexp")
        hg_hi, hg_ready = sem("hg_hi"), sem("hg_ready")
        x2_hi = sem("x2_hi")
        downed = sem("downed")
        y_hi = sem("y_hi")

        x_d = x.rearrange("(g t b) c d -> g (b c) t d", g=G, t=GT)
        out_d = out.rearrange("(g t b) c d -> g (b c) t d", g=G, t=GT)
        w_d = {"wq": wq, "wk": wk, "wv": wv, "wo": wo}
        block = ctx.enter_context(nc.Block())

        @block.sync
        def _(sp):
            def load_x(g):
                sp.dma_start(xs[:, g % XS, :, :], x_d[g]).then_inc(d_x[g], 16)

            def load_w(name, dst):
                sp.dma_start(dst, w_d[name].rearrange("(c p) k -> p c k", p=P)).then_inc(d_w[name], 16)

            with nc.allow_non_contiguous_dma(reason="512 indices, once"):
                sp.dma_start(permc[:, :], perm.rearrange("(c p) -> p c", p=P)).then_inc(d_permc, 16)
            sp.dma_start(cst[:, :], consts).then_inc(d_cst, 16)
            load_w("wq", raw_q)
            load_x(0)
            sp.wait_ge(d_wg[0], 16 * GT)
            load_w("wk", raw_k)
            load_w("wv", raw_v)
            sp.dma_start(colidx, cols.partition_broadcast(P)).then_inc(d_cols, 16)
            load_w("wo", raw_o)
            wait_prep(sp, "wq")
            sp.dma_start(raw_a, wa.rearrange("e r d -> (e r) d")).then_inc(d_lora, 16)
            for c in range(KC):
                sp.dma_start(raw_b[:, c, :, :], wb[:, P * c:P * c + P, :].rearrange("e p r -> p e r")
                             ).then_inc(d_lora, 16)
            sp.dma_start(raw_r[0:E, :], wr).then_inc(d_lora, 16)
            sp.dma_start(raw_p, perm.partition_broadcast(P)).then_inc(d_lora, 16)
            for j in range(4):
                sp.dma_start(raw_up[FD * j:FD * j + FD, :, :],
                             up.rearrange("(c j) d m -> j d c m", j=4)[j]).then_inc(d_up, 16)
            sp.dma_start(dn[:, :, :], down.rearrange("h m d -> m h d")).then_inc(d_dn, 16)
            wait_prep(sp, "wo")
            load_x(1)
            load_x(2)
            for g in range(G):
                for t in range(GT):
                    wait_read(sp, Dd(g, UN + t))
                sp.dma_start(out_d[g], xs[:, g % XS, :, :]).then_inc(d_out[g], 16)
                if g + XS < G:
                    sp.wait_ge(d_out[g], 16)
                    load_x(g + XS)
            for g in range(G):
                sp.wait_ge(d_out[g], 16)

        @block.gpsimd
        def _(pool):
            pool.memset(vz[:, :, :, :], 0.0).then_inc(vz_zero, 1)
            pool.wait_ge(idx_ready, 1)
            for t in range(TILES):
                pool.indirect_dma_start(out=wg[:, t, :], out_offset=None,
                                        in_=wcond.rearrange("s c d -> (s c) d"),
                                        in_offset=bass.IndirectOffsetOnAxis(ap=idx[:, t:t + 1], axis=0)
                                        ).then_inc(d_wg[t // GT], 16)
            pool.wait_ge(d_permc, 16)
            wait_prep(pool, "wk")
            for c in range(KC):
                pool.indirect_dma_start(out=raw_w2[:, c, :], out_offset=None, in_=w2,
                                        in_offset=bass.IndirectOffsetOnAxis(
                                            ap=permc[:, c:c + 1].bitcast(U32), axis=0)
                                        ).then_inc(d_w["w2"], 16)

            def rope(g, i):
                n = 4 * g + i
                dst = (qr, kr)[i // 2][:, 2 * (i % 2):2 * (i % 2) + 2, :].rearrange("p c (b d) -> p (c b) d", d=T)
                rv = rot[:, :, :].rearrange("p c (b d) -> p (c b) d", d=T)
                pool.wait_ge(rot_shuf, n + 1)
                pool.tensor_tensor(rv, rv, con("sin").unsqueeze(1).to_broadcast([P, 2 * N // T, T]),
                                   ALU.mult).then_inc(rot_sin, 1)
                pool.wait_ge(rot_sin, n + 1)
                wait_read(pool, A(g, (Q, K_)[i // 2] + i % 2))
                pool.tensor_tensor(dst, dst, rv, ALU.add).then_inc(roped, 1)

            def k_blocks(g, t, c):
                n = 8 * g + 4 * t + c
                if n == 1:
                    pool.wait_ge(up_ready, 4)
                pool.wait_ge(roped, 4 * g + (4 if c >= 2 else 3))
                if n >= KC:
                    wait_scored(pool, n - KC)
                kv = kr[:, c, P * t:P * t + P].rearrange("p (b s) -> p b s", b=BT)
                pool.tensor_tensor(
                    kbd[:, c, :, :].rearrange("p b (h s) -> p b h s", h=HC),
                    kv.unsqueeze(2).to_broadcast([P, BT, HC, T]),
                    con("head").unsqueeze(1).unsqueeze(3).to_broadcast([P, BT, HC, T]),
                    ALU.mult).then_inc(kbd_p, 1)

            def shift(g, i):
                n = 4 * g + i
                pool.wait_ge(maxed, n + 1)
                pool.tensor_tensor(pr[:, i, :, :], pr[:, i, :, :],
                                   mx[:, i, :].unsqueeze(2).to_broadcast([P, NH // 2, T]),
                                   ALU.subtract).then_inc(shifted, 1)

            def norm(g, i):
                n = 4 * g + i
                pool.wait_ge(recip, n + 1)
                pool.tensor_tensor(pr[:, i, :, :], pr[:, i, :, :],
                                   mx[:, i, :].unsqueeze(2).to_broadcast([P, NH // 2, T]),
                                   ALU.mult).then_inc(normed, 1)

            for i in range(4):
                rope(0, i)
            k_blocks(0, 0, 1)
            k_blocks(0, 0, 3)
            for g in range(G):
                k_blocks(g, 1, 1)
                shift(g, 0)
                shift(g, 1)
                k_blocks(g, 1, 3)
                shift(g, 2)
                shift(g, 3)
                for i in range(4):
                    norm(g, i)
                if g + 1 < G:
                    for i in range(4):
                        rope(g + 1, i)
                    k_blocks(g + 1, 0, 1)
                    k_blocks(g + 1, 0, 3)

        @block.tensor
        def _(pe):
            def mm3(dst, hi_l, lo_l, hi_r, lo_r, start, stop, skip=False):
                pe.matmul(dst, hi_l, hi_r, start=start, stop=False, skip_group_check=skip)
                pe.matmul(dst, hi_l, lo_r, start=False, stop=False, skip_group_check=skip)
                return pe.matmul(dst, lo_l, hi_r, start=False, stop=stop, skip_group_check=skip)

            def prep_w(name, raw):
                pe.wait_ge(d_w[name], 64 if name == "w2" else 16)
                if name == "wq":
                    pe.wait_ge(d_cst, 16)
                for k in range(KC):
                    it = prep(name, k)
                    wait_free(pe, it)
                    for c in range(KC):
                        last = pe.transpose(bank(it)[:, P * c:P * c + P], raw[:, c, P * k:P * k + P], ident)
                    last.then_inc(s_full(it), 1)

            def cond(g, t):
                pe.wait_ge(d_x[g], 16)
                pe.wait_ge(wbd_ready, g + 1)
                it = A(g, COND + t)
                wait_free(pe, it)
                for c in range(KC):
                    last = pe.matmul(bank(it)[:, P * c:P * c + P], xs[:, g % XS, t, P * c:P * c + P],
                                     wbd[:, t, :, :], start=True, stop=True)
                last.then_inc(s_full(it), 1)

            def qk(g, name, first, i):
                W = WT[name]
                if name == "wq" and i == 0:
                    for t in range(GT):
                        wait_read(pe, A(g, COND + t))
                it = A(g, first + i)
                wait_free(pe, it)
                for h in range(2):
                    c = 2 * i + h
                    for k in range(KC):
                        last = mm3(bank(it)[:, N * h:N * h + N],
                                   W[:, 0, k, P * c:P * c + P], W[:, 1, k, P * c:P * c + P],
                                   xc[:, 0, k, :], xc[:, 1, k, :], k == 0, k == KC - 1)
                last.then_inc(s_full(it), 1)

            def v(g, t):
                it = A(g, V + t)
                wait_free(pe, it)
                W = WT["wv"]
                for k in range(KC):
                    last = mm3(bank(it)[:, :], xc[:, 0, k, P * t:P * t + P], xc[:, 1, k, P * t:P * t + P],
                               W[:, 0, k, :], W[:, 1, k, :], k == 0, k == KC - 1)
                last.then_inc(s_full(it), 1)

            def scores(g, i):
                t, half = i // 2, i % 2
                it = S_scores(g, i)
                wait_free(pe, it)
                pe.wait_ge(roped, 4 * g + 4)
                for c in (2 * half, 2 * half + 1):
                    n = 8 * g + 4 * t + c
                    pe.wait_ge((kbd_v, kbd_p)[c % 2], n // 2 + 1)
                    for b in range(BT):
                        at = P * t + T * b
                        last = pe.matmul(bank(it)[T * b:T * b + T, N * (c % 2):N * (c % 2) + N],
                                         qr[:, c, at:at + T], kbd[:, c, b, :], start=True, stop=True)
                    last.then_inc(scored if c % 2 == 0 else s_full(it), 1)

            def pv(g, t, c):
                it = C(g, PV + t)
                if c == 0:
                    wait_free(pe, it)
                    wait_read(pe, A(g, V + t))
                n = 8 * g + 4 * t + c
                pe.wait_ge(pbd_v, n + 1)
                pe.wait_ge(pbd_a, n + 1)
                for e in range(2):
                    for j in range(4):
                        last = pe.matmul(bank(it)[32 * j:32 * j + 32, P * c:P * c + P],
                                         vz[:, t, 4 * c + j, HD * e:HD * e + 2 * HD],
                                         pbd[:, c % 2, 2 * j + e, :, :],
                                         start=(e == 0), stop=(e == 1), skip_group_check=True)
                last.then_inc(pv_done if c < KC - 1 else s_full(it), 1)

            def wo_proj(g, t):
                it = C(g, WO + t)
                wait_free(pe, it)
                wait_read(pe, C(g, PV + t))
                W = WT["wo"]
                for k in range(KC):
                    last = mm3(bank(it)[:, :], y2[:, 0, k, P * t:P * t + P], y2[:, 1, k, P * t:P * t + P],
                               W[:, 0, k, :], W[:, 1, k, :], k == 0, k == KC - 1)
                last.then_inc(s_full(it), 1)

            def turn_x1(g, t):
                it = C(g, XT + t)
                wait_free(pe, it)
                wait_read(pe, C(g, WO + t))
                for c in range(KC):
                    last = pe.transpose(bank(it)[:, P * c:P * c + P], xs[:, g % XS, t, P * c:P * c + P], ident)
                last.then_inc(s_full(it), 1)

            def lora_down(g):
                it = C(g, LH)
                wait_free(pe, it)
                for t in range(GT):
                    wait_read(pe, C(g, XT + t))
                for k in range(KC):
                    mm3(bank(it)[:, 0:N], aT[:, 0, k, :], aT[:, 1, k, :], x1[:, 0, k, :], x1[:, 1, k, :],
                        k == 0, k == KC - 1)
                for k in range(KC):
                    last = mm3(bank(it)[0:E, N:2 * N], rT[:, 0, k, :], rT[:, 1, k, :],
                               x1[:, 0, k, :], x1[:, 1, k, :], k == 0, k == KC - 1)
                last.then_inc(s_full(it), 1)

            def turn_logits(g):
                it = C(g, LT)
                wait_free(pe, it)
                wait_read(pe, C(g, LH))
                for t in range(GT):
                    last = pe.transpose(bank(it)[:, E * t:E * t + E], lg[:, P * t:P * t + P], ident[0:E, 0:E])
                last.then_inc(s_full(it), 1)

            def turn_gates(g):
                it = C(g, GTR)
                wait_free(pe, it)
                pe.wait_ge(gex_ready, g + 1)
                for t in range(GT):
                    last = pe.transpose(bank(it)[:, P * t:P * t + P],
                                        gex[:, t, :, :].rearrange("p e r -> p (e r)"), ident)
                last.then_inc(s_full(it), 1)

            def experts_base(g, i):
                it = Dd(g, W_ + i)
                wait_free(pe, it)
                W = WT["w2"]
                for h in range(2):
                    c = 2 * i + h
                    for k in range(KC):
                        mm3(bank(it)[:, N * h:N * h + N], W[:, 0, k, P * c:P * c + P], W[:, 1, k, P * c:P * c + P],
                            x1[:, 0, k, :], x1[:, 1, k, :], h == 0 and k == 0, False, skip=True)

            def experts_lora(g, i):
                it = Dd(g, W_ + i)
                pe.wait_ge(hg_ready, g + 1)
                for h in range(2):
                    c = 2 * i + h
                    last = mm3(bank(it)[:, N * h:N * h + N], bT[:, 0, P * c:P * c + P], bT[:, 1, P * c:P * c + P],
                               hg[:, 0, :], hg[:, 1, :], False, h == 1, skip=True)
                last.then_inc(s_full(it), 1)

            def ffn_up(g, i):
                it = Dd(g, UP + i)
                wait_free(pe, it)
                wait_read(pe, Dd(g, W_ + i // 4))
                c = i // 2
                for h in range(2):
                    j = 2 * (i % 2) + h
                    last = mm3(bank(it)[:, N * h:N * h + N], upP[:, 0, c, j, :], upP[:, 1, c, j, :],
                               y2[:, 0, c, :], y2[:, 1, c, :], True, True)
                last.then_inc(s_full(it), 1)

            def ffn_down(g, c):
                it = S_down(g, c // 2)
                if c % 2 == 0:
                    wait_free(pe, it)
                for i in range(2):
                    wait_read(pe, Dd(g, UP + 2 * c + i))
                for j in range(4):
                    last = pe.matmul(bank(it)[32 * j:32 * j + 32, N * (c % 2):N * (c % 2) + N],
                                     dn[:, 4 * c + j, :], act[:, (2 * c + j // 2) % 4, j % 2, :],
                                     start=True, stop=True)
                last.then_inc(downed if c % 2 == 0 else s_full(it), 1)

            def unpermute(g, t):
                it = Dd(g, UN + t)
                wait_free(pe, it)
                for i in range(2):
                    wait_read(pe, S_down(g, i))
                for c in range(KC):
                    for part in range(2):
                        last = pe.matmul(bank(it)[:, :], y2[:, part, c, P * t:P * t + P], unperm[:, c, :],
                                         start=(c == 0 and part == 0), stop=(c == KC - 1 and part == 1))
                last.then_inc(s_full(it), 1)

            def ffn(g):
                for i in range(4):
                    ffn_up(g, i)
                ffn_down(g, 0)
                ffn_up(g, 4)
                ffn_up(g, 5)
                ffn_down(g, 1)
                ffn_up(g, 6)
                ffn_up(g, 7)
                ffn_down(g, 2)
                ffn_down(g, 3)

            def prep_b():
                it = prep("b")
                wait_free(pe, it)
                pe.wait_ge(d_lora, 16 * (3 + KC))
                pe.wait_ge(pick_ready, KC)
                for c in range(KC):
                    last = pe.matmul(bank(it)[:, :], raw_b[:, c, :, :].rearrange("p e r -> p (e r)"),
                                     pick[:, c, :], start=(c == 0), stop=(c == KC - 1))
                last.then_inc(s_full(it), 1)

            def prep_ar():
                for name, raw, n in (("a", raw_a, P), ("r", raw_r[0:E, :], E)):
                    it = prep(name)
                    wait_free(pe, it)
                    for k in range(KC):
                        last = pe.transpose(bank(it)[:, n * k:n * k + n], raw[:, P * k:P * k + P],
                                            ident[0:n, 0:n])
                    last.then_inc(s_full(it), 1)

            prep_w("wq", raw_q)
            cond(0, 0)
            cond(0, 1)
            prep_w("wk", raw_k)
            wait_prep(pe, "wq")
            qk(0, "wq", Q, 0)
            prep_w("wv", raw_v)
            qk(0, "wq", Q, 1)
            wait_prep(pe, "wk")
            qk(0, "wk", K_, 0)
            prep_w("w2", raw_w2)
            qk(0, "wk", K_, 1)
            prep_w("wo", raw_o)
            prep_b()
            wait_prep(pe, "wv")
            v(0, 0)
            scores(0, 0)
            scores(0, 1)
            prep_ar()
            v(0, 1)
            cond(1, 0)
            cond(1, 1)
            for g in range(G):
                if g:
                    if g + 1 < G:
                        cond(g + 1, 0)
                    scores(g, 0)
                    scores(g, 1)
                    lora_down(g - 1)
                scores(g, 2)
                if g:
                    turn_logits(g - 1)
                    experts_base(g - 1, 0)
                    experts_base(g - 1, 1)
                    turn_gates(g - 1)
                scores(g, 3)
                if g:
                    experts_lora(g - 1, 0)
                    experts_lora(g - 1, 1)
                    if g + 1 < G:
                        cond(g + 1, 1)
                    ffn(g - 1)
                if g + 1 < G:
                    qk(g + 1, "wq", Q, 0)
                if g:
                    pv(g, 0, 0)
                    unpermute(g - 1, 0)
                    pv(g, 0, 1)
                    unpermute(g - 1, 1)
                    pv(g, 0, 2)
                if g + 1 < G:
                    qk(g + 1, "wq", Q, 1)
                if g == 0:
                    pv(g, 0, 0)
                    pv(g, 0, 1)
                else:
                    pv(g, 0, 3)
                if g + 1 < G:
                    qk(g + 1, "wk", K_, 0)
                if g == 0:
                    pv(g, 0, 2)
                else:
                    pv(g, 1, 0)
                if g + 1 < G:
                    qk(g + 1, "wk", K_, 1)
                if g == 0:
                    pv(g, 0, 3)
                    pv(g, 1, 0)
                pv(g, 1, 1)
                if g + 1 < G:
                    v(g + 1, 0)
                pv(g, 1, 2)
                pv(g, 1, 3)
                if g == 0:
                    wait_prep(pe, "wo")
                wo_proj(g, 0)
                if g + 1 < G:
                    v(g + 1, 1)
                wo_proj(g, 1)
                turn_x1(g, 0)
                turn_x1(g, 1)
                if g == 0:
                    wait_prep(pe, "r", 1)
                    pe.wait_ge(up_ready, 4)
                    pe.wait_ge(unperm_ready, KC)
                    pe.wait_ge(d_dn, 16)
            lora_down(G - 1)
            turn_logits(G - 1)
            experts_base(G - 1, 0)
            experts_base(G - 1, 1)
            turn_gates(G - 1)
            experts_lora(G - 1, 0)
            experts_lora(G - 1, 1)
            ffn(G - 1)
            unpermute(G - 1, 0)
            unpermute(G - 1, 1)

        @block.scalar
        def _(sc):
            def copy(dst, src):
                return sc.activation(dst, src, ACT.Copy)

            def prep_his(name, n, dst):
                for k in range(n):
                    it = prep(name, k)
                    wait_full(sc, it)
                    copy(dst(k), bank(it)[:, 0:dst(k).free_size()]).then_inc(prep_hi, 1)

            def cond_hi(g, t):
                it = A(g, COND + t)
                wait_full(sc, it)
                copy(xc[:, 0, :, P * t:P * t + P], bank(it)[:, :].rearrange("p (c n) -> p c n", c=KC)
                     ).then_inc(xc_hi, 1)

            def v_out(g, t):
                it = A(g, V + t)
                if g == 0 and t == 0:
                    sc.wait_ge(vz_zero, 1)
                wait_full(sc, it)
                dst = vz[:, t, :, :].rearrange("p q (s f) -> p q s f", f=HD)[:, :, 0:3:2, :]
                copy(dst, bank(it)[:, :].rearrange("p (q s f) -> p q s f", s=2, f=HD)).then_inc(s_free(it), 1)

            def exp(g, i):
                sc.wait_ge(shifted, 4 * g + i + 1)
                sc.activation(pr[:, i, :, :], pr[:, i, :, :], ACT.Exp, scale=float(HD) ** -0.5
                              ).then_inc(exped, 1)

            def gate_exp(g):
                sc.wait_ge(gap, g + 1)
                sc.activation(e2, e2, ACT.Exp).then_inc(gexp, 1)

            def gelu_table(g):
                sc.activation(unused[:, g:g + 1], con("pos"), ACT.Gelu)

            def h_out(g):
                it = C(g, LH)
                wait_full(sc, it)
                copy(hs, bank(it)[:, 0:N]).then_inc(h_ready, 1)

            def probs_block(g, t, c):
                n = 8 * g + 4 * t + c
                sc.wait_ge(turned, 4 * g + 2 * t + c // 2 + 1)
                if n >= 2:
                    wait_pv(sc, n - 2)
                if n == 0:
                    wait_prep(sc, "r", 1)
                src = pT(2 * t + c // 2)[:, HC * (c % 2):HC * (c % 2) + HC, :]
                b = BT - 1
                sc.activation(pbd[:, c % 2, :, b, :], src, ACT.Copy, scale=con("seq")[:, b:b + 1]
                              ).then_inc(pbd_a, 1)

            def split_hi(it, dst, s):
                wait_full(sc, it)
                copy(dst, bank(it)[:, :].rearrange("p (c n) -> p c n", n=dst.shape[-1])).then_inc(s, 1)

            def gelu(g, i):
                it = Dd(g, UP + i)
                n = 8 * g + i
                wait_full(sc, it)
                if n >= 4:
                    wait_down(sc, (n - 4) // 8, (n - 4) % 8 // 2)
                sc.activation(act[:, i % 4, :, :], bank(it)[:, :].rearrange("p (h n) -> p h n", h=2), ACT.Gelu
                              ).then_inc(s_free(it), 1)

            def x2_his(g):
                for i in range(2):
                    split_hi(Dd(g, W_ + i), y2[:, 0, 2 * i:2 * i + 2, :], x2_hi)

            def ffn(g):
                for i in range(6):
                    gelu(g, i)
                split_hi(S_down(g, 0), y2[:, 0, 0:2, :], y_hi)
                gelu(g, 6)
                gelu(g, 7)
                split_hi(S_down(g, 1), y2[:, 0, 2:4, :], y_hi)

            sc.dma_start(ids[:, 0, :], subj.partition_broadcast(P)).then_inc(d_ids, 16)
            sc.dma_start(ids[:, 1, :], lang.partition_broadcast(P)).then_inc(d_ids, 16)
            prep_his("wq", KC, lambda k: WT["wq"][:, 0, k, :])
            cond_hi(0, 0)
            cond_hi(0, 1)
            prep_his("wk", KC, lambda k: WT["wk"][:, 0, k, :])
            prep_his("wv", KC, lambda k: WT["wv"][:, 0, k, :])
            sc.wait_ge(d_up, 64)
            for j in range(4):
                sc.activation(upP[:, 0, :, j, :], raw_up, ACT.Copy, scale=con("seq")[:, j:j + 1]
                              ).then_inc(up_hi, 1)
            prep_his("w2", KC, lambda k: WT["w2"][:, 0, k, :])
            prep_his("wo", KC, lambda k: WT["wo"][:, 0, k, :])
            prep_his("b", 1, lambda k: bT[:, 0, :])
            v_out(0, 0)
            prep_his("a", 1, lambda k: aT[:, 0, :, :].rearrange("p a b -> p (a b)"))
            prep_his("r", 1, lambda k: rT[:, 0, :, :].rearrange("p a b -> p (a b)"))
            v_out(0, 1)
            cond_hi(1, 0)
            cond_hi(1, 1)
            for g in range(G):
                if g and g + 1 < G:
                    cond_hi(g + 1, 0)
                if g:
                    h_out(g - 1)
                exp(g, 0)
                exp(g, 1)
                if g:
                    gate_exp(g - 1)
                    gelu_table(g - 1)
                    x2_his(g - 1)
                    if g + 1 < G:
                        cond_hi(g + 1, 1)
                    ffn(g - 1)
                exp(g, 2)
                exp(g, 3)
                for c in range(KC):
                    probs_block(g, 0, c)
                probs_block(g, 1, 0)
                split_hi(C(g, PV), y2[:, 0, :, 0:P], o_hi)
                probs_block(g, 1, 1)
                probs_block(g, 1, 2)
                probs_block(g, 1, 3)
                if g + 1 < G:
                    v_out(g + 1, 0)
                split_hi(C(g, PV + 1), y2[:, 0, :, P:2 * P], o_hi)
                if g + 1 < G:
                    v_out(g + 1, 1)
                for t in range(GT):
                    split_hi(C(g, XT + t), x1[:, 0, :, P * t:P * t + P], x1_hi)
            h_out(G - 1)
            gate_exp(G - 1)
            gelu_table(G - 1)
            x2_his(G - 1)
            ffn(G - 1)

        @block.vector
        def _(ve):
            steps = [0]

            def step(ins):
                steps[0] += 1
                ins.then_inc(setup, 1)
                ve.wait_ge(setup, steps[0])

            def split_lo(it, hi, lo, s_hi, n_hi):
                ve.wait_ge(s_hi, n_hi)
                src = bank(it)[:, 0:hi.free_size()]
                if len(hi.shape) == 3:
                    src = src.rearrange("p (c n) -> p c n", n=hi.shape[-1])
                wait_full(ve, it)
                ve.tensor_tensor(lo, src, hi.bitcast(F32), ALU.subtract).then_inc(s_free(it), 1)

            def prep_los(name, n, w):
                for k in range(n):
                    it = prep(name, k)
                    split_lo(it, w(k, 0), w(k, 1), prep_hi, PREP[name] + k + 1)

            def cond_lo(g, t):
                at = slice(P * t, P * t + P)
                split_lo(A(g, COND + t), xc[:, 0, :, at], xc[:, 1, :, at], xc_hi, GT * g + t + 1)

            def blocks(g):
                ve.wait_ge(d_wg[g], 16 * GT)
                if g:
                    wait_full(ve, A(g - 1, COND + 1))
                for b in range(BT):
                    i = ve.tensor_scalar(wbd[:, :, b, :], wg[:, GT * g:GT * g + GT, :],
                                         con("seq")[:, b:b + 1], None, ALU.mult)
                i.then_inc(wbd_ready, 1)

            def rope(g, i):
                n = 4 * g + i
                it = A(g, (Q, K_)[i // 2] + i % 2)
                dst = (qr, kr)[i // 2][:, 2 * (i % 2):2 * (i % 2) + 2, :].rearrange("p c (b d) -> p (c b) d", d=T)
                src = bank(it)[:, :]
                wait_full(ve, it)
                if n:
                    ve.wait_ge(roped, n)
                half = HD // 2
                order = [(j + half) if j % HD < half else (j - half) for j in range(32)]
                ve.stream_shuffle(rot[:, :, :].rearrange("p c n -> p (c n)"), src, order).then_inc(rot_shuf, 1)
                ve.tensor_tensor(dst, src.rearrange("p (c d) -> p c d", d=T),
                                 con("cos").unsqueeze(1).to_broadcast([P, 2 * N // T, T]), ALU.mult
                                 ).then_inc(s_free(it), 1)

            def k_blocks(g, t, c):
                n = 8 * g + 4 * t + c
                ve.wait_ge(roped, 4 * g + (4 if c >= 2 else 3))
                if n >= KC:
                    wait_scored(ve, n - KC)
                if n == 0:
                    ve.wait_ge(up_ready, 4)
                kv = kr[:, c, P * t:P * t + P].rearrange("p (b s) -> p b s", b=BT)
                ve.tensor_tensor(
                    kbd[:, c, :, :].rearrange("p b (h s) -> p b h s", h=HC),
                    kv.unsqueeze(2).to_broadcast([P, BT, HC, T]),
                    con("head").unsqueeze(1).unsqueeze(3).to_broadcast([P, BT, HC, T]),
                    ALU.mult).then_inc(kbd_v, 1)

            def mask(g, i):
                it = S_scores(g, i)
                n = 4 * g + i
                wait_full(ve, it)
                if n == 0:
                    wait_prep(ve, "b", 1)
                ve.tensor_tensor(pr[:, i, :, :], bank(it)[:, :].rearrange("p (h s) -> p h s", s=T),
                                 con("causal").unsqueeze(1).to_broadcast([P, NH // 2, T]), ALU.add
                                 ).then_inc(s_free(it), 1)

            def row_max(g, i):
                wait_read(ve, S_scores(g, i))
                ve.tensor_reduce(mx[:, i, :], pr[:, i, :, :], AX_X, ALU.max).then_inc(maxed, 1)

            def mask_max(g, i):
                mask(g, i)
                row_max(g, i)

            def sums(g, i):
                n = 4 * g + i
                ve.wait_ge(exped, n + 1)
                ve.tensor_reduce(sm[:, i, :], pr[:, i, :, :], AX_X, ALU.add).then_inc(summed, 1)
                ve.wait_ge(summed, n + 1)
                ve.reciprocal(mx[:, i, :], sm[:, i, :]).then_inc(recip, 1)

            def turn(g, i):
                ve.wait_ge(normed, 4 * g + i + 1)
                if g == 0 and i == 0:
                    ve.wait_ge(unperm_ready, KC)
                if i:
                    ve.wait_ge(turned, 4 * g + i)
                ve.transpose(pT(i), pr[:, i, :, :]).then_inc(turned, 1)

            def probs_blocks(g, t, c):
                n = 8 * g + 4 * t + c
                ve.wait_ge(turned, 4 * g + 2 * t + c // 2 + 1)
                if n >= 2:
                    wait_pv(ve, n - 2)
                if n == 0:
                    wait_prep(ve, "r", 1)
                src = pT(2 * t + c // 2)[:, HC * (c % 2):HC * (c % 2) + HC, :]
                for b in range(BT - 1):
                    i = ve.tensor_scalar(pbd[:, c % 2, :, b, :], src, con("seq")[:, b:b + 1], None, ALU.mult)
                i.then_inc(pbd_v, 1)

            def o_lo(g, t):
                at = slice(P * t, P * t + P)
                split_lo(C(g, PV + t), y2[:, 0, :, at], y2[:, 1, :, at], o_hi, GT * g + t + 1)

            def add_x(g, t):
                it = C(g, WO + t)
                wait_full(ve, it)
                ve.tensor_tensor(xs[:, g % XS, t, :], bank(it)[:, :], xs[:, g % XS, t, :], ALU.add
                                 ).then_inc(s_free(it), 1)

            def x1_lo(g, t):
                at = slice(P * t, P * t + P)
                split_lo(C(g, XT + t), x1[:, 0, :, at], x1[:, 1, :, at], x1_hi, GT * g + t + 1)

            def logits_out(g):
                it = C(g, LH)
                wait_full(ve, it)
                ve.wait_ge(h_ready, g + 1)
                ve.tensor_copy(lg, bank(it)[0:E, N:2 * N]).then_inc(s_free(it), 1)

            gsteps = [0]

            def gate(ins):
                gsteps[0] += 1
                ins.then_inc(gstep, 1)
                ve.wait_ge(gstep, gsteps[0])

            def gates(g):
                it = C(g, LT)
                wide = [P, GT, E]

                def w(v):
                    return v.unsqueeze(2).to_broadcast(wide)

                experts_, experts16 = (con(n).unsqueeze(1).to_broadcast(wide) for n in ("expert", "expert16"))
                wait_full(ve, it)
                ve.tensor_tensor(L, bank(it)[:, 0:GT * E].rearrange("p (t e) -> p t e", t=GT),
                                 bias[:, GT * g:GT * g + GT, :], ALU.add).then_inc(s_free(it), 1)
                wait_read(ve, it)
                for src, m, oh in ((L, m1, oh1), (L2, m2, oh2)):
                    gate(ve.tensor_reduce(m, src, AX_X, ALU.max))
                    gate(ve.tensor_tensor(eq, src, w(m), ALU.is_equal))
                    gate(ve.scalar_tensor_tensor(out=cand, in0=eq, scalar=-16.0, in1=experts16,
                                                 op0=ALU.mult, op1=ALU.add))
                    gate(ve.tensor_reduce(i1, cand, AX_X, ALU.min))
                    gate(ve.tensor_tensor(oh, experts_, w(i1), ALU.is_equal))
                    if oh is oh1:
                        gate(ve.scalar_tensor_tensor(out=L2, in0=oh1, scalar=NEVER, in1=L,
                                                     op0=ALU.mult, op1=ALU.add))
                ve.tensor_tensor(e2, m2, m1, ALU.subtract).then_inc(gap, 1)
                ve.wait_ge(gexp, g + 1)
                gate(ve.tensor_scalar(g2, e2, 1.0, None, ALU.add))
                gate(ve.reciprocal(g1, g2))
                gate(ve.tensor_tensor(g2, e2, g1, ALU.mult))
                gate(ve.tensor_tensor(oh1, oh1, w(g1), ALU.mult))
                gate(ve.tensor_tensor(oh2, oh2, w(g2), ALU.mult))
                gate(ve.tensor_tensor(cand, oh1, oh2, ALU.add))
                ve.tensor_scalar(gex, cand.unsqueeze(3).to_broadcast([P, GT, E, R]), SCALING, None,
                                 ALU.mult).then_inc(gex_ready, 1)

            def gate_h(g):
                it = C(g, GTR)
                wait_full(ve, it)
                ve.wait_ge(h_ready, g + 1)
                ve.tensor_tensor(hgf, bank(it)[:, 0:N], hs, ALU.mult).then_inc(s_free(it), 1)
                wait_read(ve, it)
                ve.tensor_copy(hg[:, 0, :], hgf).then_inc(hg_hi, 1)
                ve.wait_ge(hg_hi, g + 1)
                ve.tensor_tensor(hg[:, 1, :], hgf, hg[:, 0, :].bitcast(F32), ALU.subtract).then_inc(hg_ready, 1)

            def x2_lo(g, i):
                at = slice(2 * i, 2 * i + 2)
                split_lo(Dd(g, W_ + i), y2[:, 0, at, :], y2[:, 1, at, :], x2_hi, 2 * g + i + 1)

            def y_lo(g, i):
                at = slice(2 * i, 2 * i + 2)
                split_lo(S_down(g, i), y2[:, 0, at, :], y2[:, 1, at, :], y_hi, 2 * g + i + 1)

            def add_ffn(g, t):
                it = Dd(g, UN + t)
                wait_full(ve, it)
                ve.tensor_tensor(xs[:, g % XS, t, :], bank(it)[:, :], xs[:, g % XS, t, :], ALU.add
                                 ).then_inc(s_free(it), 1)

            ve.wait_ge(d_ids, 32)
            ve.wait_ge(d_cst, 16)
            for b in range(BT):
                at = slice(T * b, T * b + T)
                i = ve.tensor_scalar(idx[at, :], ids[at, 0, b:B:BT], float(T), con("pos")[at, :],
                                     ALU.mult, ALU.add)
            i.then_inc(idx_ready, 1)
            for b in range(BT):
                at = slice(T * b, T * b + T)
                i = ve.tensor_copy(langf[at, :], ids[at, 1, b:B:BT])
            step(i)
            ve.wait_ge(d_permc, 16)
            ve.tensor_copy(permf, permc[:, :]).then_inc(permf_ready, 1)
            step(ve.tensor_tensor(bias, con("expert").unsqueeze(1).to_broadcast([P, TILES, E]),
                                  langf.unsqueeze(2).to_broadcast([P, TILES, E]), ALU.is_equal))
            step(ve.tensor_scalar(bias, bias, LANG_BIAS, None, ALU.mult))
            prep_los("wq", KC, lambda k, s: WT["wq"][:, s, k, :])
            blocks(0)
            cond_lo(0, 0)
            cond_lo(0, 1)
            prep_los("wk", KC, lambda k, s: WT["wk"][:, s, k, :])
            blocks(1)
            rope(0, 0)
            prep_los("wv", KC, lambda k, s: WT["wv"][:, s, k, :])
            wait_prep(ve, "wv")
            ve.wait_ge(d_lora, 16 * (3 + KC))
            for c in range(KC):
                ve.tensor_scalar(pick[:, c, :], raw_p, con("row")[:, c:c + 1], None, ALU.is_equal
                                 ).then_inc(pick_ready, 1)
            rope(0, 1)
            for j in range(4):
                ve.wait_ge(up_hi, j + 1)
                ve.scalar_tensor_tensor(out=upP[:, 1, :, j, :], in0=raw_up, scalar=con("seq")[:, j:j + 1],
                                        in1=upP[:, 0, :, j, :].bitcast(F32), op0=ALU.mult, op1=ALU.subtract
                                        ).then_inc(up_ready, 1)
            rope(0, 2)
            prep_los("w2", KC, lambda k, s: WT["w2"][:, s, k, :])
            rope(0, 3)
            prep_los("wo", KC, lambda k, s: WT["wo"][:, s, k, :])
            k_blocks(0, 0, 0)
            k_blocks(0, 0, 2)
            prep_los("b", 1, lambda k, s: bT[:, s, :])
            ve.wait_ge(permf_ready, 1)
            ve.wait_ge(d_cols, 16)
            for c in range(KC):
                ve.tensor_scalar(unperm[:, c, :], colidx, permf[:, c:c + 1], None, ALU.is_equal
                                 ).then_inc(unperm_ready, 1)
            for g in range(G):
                if g and g + 1 < G:
                    cond_lo(g + 1, 0)
                mask_max(g, 0)
                k_blocks(g, 1, 0)
                mask_max(g, 1)
                if g == 0:
                    k_blocks(0, 1, 2)
                    prep_los("a", 1, lambda k, s: aT[:, s, :, :].rearrange("p a b -> p (a b)"))
                    prep_los("r", 1, lambda k, s: rT[:, s, :, :].rearrange("p a b -> p (a b)"))
                    cond_lo(1, 0)
                    cond_lo(1, 1)
                if g:
                    logits_out(g - 1)
                    gates(g - 1)
                    k_blocks(g, 1, 2)
                    gate_h(g - 1)
                mask_max(g, 2)
                if g:
                    x2_lo(g - 1, 0)
                    x2_lo(g - 1, 1)
                    if g + 1 < G:
                        cond_lo(g + 1, 1)
                mask_max(g, 3)
                if g + 2 < G:
                    blocks(g + 2)
                sums(g, 0)
                sums(g, 1)
                turn(g, 0)
                turn(g, 1)
                probs_blocks(g, 0, 0)
                if g:
                    y_lo(g - 1, 0)
                    probs_blocks(g, 0, 1)
                    y_lo(g - 1, 1)
                    sums(g, 2)
                else:
                    sums(g, 2)
                    probs_blocks(g, 0, 1)
                sums(g, 3)
                if g + 1 < G:
                    rope(g + 1, 0)
                turn(g, 2)
                turn(g, 3)
                probs_blocks(g, 0, 2)
                if g:
                    add_ffn(g - 1, 0)
                    probs_blocks(g, 0, 3)
                    add_ffn(g - 1, 1)
                    if g + 1 < G:
                        rope(g + 1, 1)
                    probs_blocks(g, 1, 0)
                    if g + 1 < G:
                        rope(g + 1, 2)
                    o_lo(g, 0)
                    probs_blocks(g, 1, 1)
                    probs_blocks(g, 1, 2)
                    if g + 1 < G:
                        rope(g + 1, 3)
                else:
                    rope(1, 1)
                    probs_blocks(g, 0, 3)
                    rope(1, 2)
                    probs_blocks(g, 1, 0)
                    rope(1, 3)
                    o_lo(g, 0)
                    probs_blocks(g, 1, 1)
                    probs_blocks(g, 1, 2)
                probs_blocks(g, 1, 3)
                o_lo(g, 1)
                add_x(g, 0)
                if g + 1 < G:
                    k_blocks(g + 1, 0, 0)
                    k_blocks(g + 1, 0, 2)
                add_x(g, 1)
                x1_lo(g, 0)
                x1_lo(g, 1)
            logits_out(G - 1)
            gates(G - 1)
            gate_h(G - 1)
            x2_lo(G - 1, 0)
            x2_lo(G - 1, 1)
            y_lo(G - 1, 0)
            y_lo(G - 1, 1)
            add_ffn(G - 1, 0)
            add_ffn(G - 1, 1)


_INS = ["x", "itok_B_0_30", "itok_B_0_7", "L0_cond_weights", "L0_attn_wq", "L0_attn_wk", "L0_attn_wv",
        "L0_attn_wo", "L0_cond2_W", "L0_cond2_Wr", "L0_cond2_A", "L0_cond2_B", "L0_ffn_up", "L0_ffn_down",
        "L0_ffn_perm"]


def kernel(**inputs):
    import concourse.bacc as _bacc
    from concourse.bass_utils import run_bass_kernel_spmd as _run

    nc = _bacc.Bacc("TRN2", target_bir_lowering=False, num_devices=1,
                     dynamic_dma_scratch_size=4096)
    arrays, args = {}, []

    def give(name, a):
        a = np.ascontiguousarray(a)
        arrays[name] = a
        args.append(nc.dram_tensor(name, a.shape, mybir.dt.from_np(a.dtype), kind="ExternalInput").ap())

    for name in _INS:
        give(f"in_{name}", inputs[name])
    give("constants", constants())
    give("columns", np.arange(D, dtype=np.float32))
    args.append(nc.dram_tensor("out_0", (B, T, D), F32, kind="ExternalOutput").ap())
    build(nc, *args)
    r = _run(nc, [arrays], core_ids=[0])
    return r.results[0]["out_0"]
```

```python
from contextlib import ExitStack

import numpy as np

import concourse.bass as bass
from concourse import mybir

F32 = mybir.dt.float32
F32R = mybir.dt.float32r
I32 = mybir.dt.int32
U32 = mybir.dt.uint32
ALU = mybir.AluOpType
ACT = mybir.ActivationFunctionType
AX_X = mybir.AxisListType.X

P = 128
B, T, D = 32, 32, 512
NH, HD = 32, 16
E, R = 8, 16
FH, FD, FM = 16, 32, 128
LANG_BIAS, SCALING = 5.0, 2.0
KC = D // P
TILES = B * T // P
BT = P // T
GT = 2
G = TILES // GT
N = GT * P
HC = P // HD
XS = 3
MASKED = -1.0e30
NEVER = -3.0e38

_AT = {}
_W = 0
for _name, _n in [("ident", P), ("cos", T), ("sin", T), ("causal", T), ("head", HC), ("seq", BT),
                  ("row", KC), ("pos", 1), ("expert", E), ("expert16", E)]:
    _AT[_name] = (_W, _W + _n)
    _W += _n
CW = _W


def constants():
    p = np.arange(P)
    c = np.zeros((P, CW), np.float32)

    def put(name, v):
        c[:, _AT[name][0]:_AT[name][1]] = v

    put("ident", np.eye(P))
    pos = np.arange(T, dtype=np.float32)
    theta = (np.float32(1.0) / np.float32(10000.0) ** (np.arange(0, HD, 2, dtype=np.float32) / np.float32(HD)))
    angle = np.outer(pos, theta.astype(np.float32)).astype(np.float32)
    by_row = angle[:, (p % HD) % (HD // 2)].T
    put("cos", np.cos(by_row))
    put("sin", np.where((p % HD < HD // 2)[:, None], -np.sin(by_row), np.sin(by_row)))
    put("causal", np.where(np.arange(T)[None] <= (p % T)[:, None], 0.0, MASKED))
    put("head", (p // HD)[:, None] == np.arange(HC)[None])
    put("seq", (p // T)[:, None] == np.arange(BT)[None])
    put("row", p[:, None] + P * np.arange(KC)[None])
    put("pos", (p % T)[:, None])
    put("expert", np.arange(E)[None])
    put("expert16", np.arange(E)[None] + 16)
    return c


def build(nc, x, subj, lang, wcond, wq, wk, wv, wo, w2, wr, wa, wb, up, down, perm, consts, out):
    ctx = ExitStack()
    with ctx:
        def sb(name, shape, dt=F32):
            return ctx.enter_context(nc.sbuf_tensor(name, shape, dt))

        def sem(name):
            return ctx.enter_context(nc.semaphore(name))

        WT = {n: sb(f"{n}T", [P, 2, KC, D], F32R) for n in ("wq", "wk", "wv", "wo", "w2")}
        aT = sb("aT", [P, 2, KC, P], F32R)
        rT = sb("rT", [P, 2, KC, E], F32R)
        bT = sb("bT", [P, 2, D], F32R)
        upP = sb("upP", [P, 2, KC, 4, FM], F32R)
        dn = sb("dn", [P, FH, FD])
        unperm = sb("unperm", [P, KC, D], F32R)
        cst = sb("cst", [P, CW])

        xs = sb("xs", [P, XS, GT, D])
        wg = sb("wg", [P, TILES, T])
        wbd = sb("wbd", [P, GT, BT, T])
        xc = sb("xc", [P, 2, KC, N], F32R)
        qr = sb("qr", [P, KC, N])
        kr = sb("kr", [P, KC, N])
        rot = sb("rot", [P, 2, N])
        kbd = sb("kbd", [P, KC, BT, HC * T])
        vz = sb("vz", [P, GT, NH // 2, 3 * HD])
        pr = sb("pr", [P, 5, NH // 2, T])
        pbd = sb("pbd", [P, 2, HC, BT, T])
        x1 = sb("x1", [P, 2, KC, N], F32R)
        y2 = sb("y2", [P, 2, KC, N], F32R)
        act = sb("act", [P, 4, 2, N])
        hg = sb("hg", [P, 2, N], F32R)
        small = sb("small", [P, 348])
        idx = sb("idx", [P, TILES], U32)
        permc = sb("permc", [P, KC], I32)
        raw_up = sb("raw_up", [P, KC, FM])[:, :, :]

        raw_q = pbd[:, :, :, :, :].rearrange("p a b c d -> p (a b c d)").rearrange("p (c k) -> p c k", c=KC)
        raw_k = act[:, :, :, :].rearrange("p a b n -> p (a b n)").rearrange("p (c k) -> p c k", c=KC)
        raw_v = pr[:, 0:4, :, :].rearrange("p a b n -> p (a b n)").rearrange("p (c k) -> p c k", c=KC)
        raw_a = raw_q[:, 0, :]
        raw_b = raw_q[:, 1, :].rearrange("p (c e r) -> p c e r", c=KC, e=E)
        raw_r = raw_q[:, 2, :]
        raw_p = raw_q[:, 3, :].bitcast(I32)
        pick = y2[:, :, :, :].rearrange("p s c n -> p (s c n)").rearrange("p (c k) -> p c k", c=KC)
        raw_o = xs[:, 1:3, :, :].rearrange("p a t d -> p (a t) d")
        raw_w2 = raw_k

        bs = x1[:, :, 0:2, :].rearrange("p s a n -> p s (a n)")

        def attn_out(g):
            return y2 if g + 1 < G else xc

        def pT(i):
            return pr[:, (i - 1) % 5, :, :]

        act_flat = act[:, :, :, :].rearrange("p a b n -> p (a b n)")
        lg = act_flat[0:E, 0:N]
        gex = act_flat[:, N:2 * N].rearrange("p (t e r) -> p t e r", t=GT, e=E)
        hs = act_flat[:, 2 * N:3 * N]
        hgf = act_flat[:, 3 * N:4 * N]

        _s = [0]

        def cut(*shape):
            n = int(np.prod(shape))
            v = small[:, _s[0]:_s[0] + n]
            _s[0] += n
            return v if len(shape) == 1 else v.rearrange("p (a b) -> p a b", a=shape[0])

        mx, sm = cut(4, NH // 2), cut(4, NH // 2)
        langf = cut(TILES)
        bias = cut(TILES, E)
        unused = cut(G)
        L, eq, cand, oh1, oh2 = (cut(GT, E) for _ in range(5))
        L2 = cut(GT, E)
        m1, m2, i1, e2, g1, g2 = (cut(GT) for _ in range(6))
        ids = sb("ids", [P, 2, B], I32)

        def con(name):
            return cst[:, _AT[name][0]:_AT[name][1]]

        ident = con("ident")

        rings = {r: [ctx.enter_context(nc.psum_tensor(f"ps_{r}{i}", [P, 512], F32)) for i in range(2)]
                 for r in "ASCD"}
        full = {r: [sem(f"{r}{i}_full") for i in range(2)] for r in "ASCD"}
        free = {r: [sem(f"{r}{i}_free") for i in range(2)] for r in "ASCD"}

        def A(g, k):
            return "A", 8 * g + k

        def S_scores(g, i):
            return "S", 4 * g + 2 * max(0, g - 1) + i

        def S_down(g, h):
            return "S", 4 * min(g + 2, G) + 2 * g + h

        def C(g, k):
            return "C", NPREP - D_PREP + 10 * g + k

        PREP = {"wq": 0, "wk": 4, "wv": 8, "wo": 12, "unperm": 16, "w2": 20, "b": 24, "a": 26, "r": 27}
        NPREP = 28

        def prep(name, k=0):
            n = PREP[name] + k
            return "DC"[n // 2 % 2], n // 4 * 2 + n % 2

        D_PREP = sum(n // 2 % 2 == 0 for n in range(NPREP))

        def Dd(g, k):
            return "D", D_PREP + 12 * g + k

        COND, Q, K_, V = 0, 2, 4, 6
        PV, WO, XT, LR, LH, LT, GTR = 0, 2, 4, 6, 7, 8, 9
        W_, UP, UN = 0, 2, 10

        def bank(item):
            r, n = item
            return rings[r][n % 2]

        def wait_free(eng, item):
            r, n = item
            if n >= 2:
                eng.wait_ge(free[r][n % 2], n // 2)

        def wait_full(eng, item):
            r, n = item
            eng.wait_ge(full[r][n % 2], n // 2 + 1)

        def wait_read(eng, item):
            r, n = item
            eng.wait_ge(free[r][n % 2], n // 2 + 1)

        def wait_prep(eng, name, n=4):
            wait_read(eng, prep(name, n - 1))

        def wait_scored(eng, n):
            if n % 2:
                wait_full(eng, S_scores(n // 8, n // 2 % 4))
            else:
                eng.wait_ge(scored, n // 2 + 1)

        def wait_pv(eng, n):
            tile, c = n // 4, n % 4
            if c == 3:
                wait_full(eng, C(tile // GT, PV + tile % GT))
            else:
                eng.wait_ge(pv_done, 3 * tile + c + 1)

        def wait_down(eng, g, c):
            if c % 2:
                wait_full(eng, S_down(g, c // 2))
            else:
                eng.wait_ge(downed, 2 * g + c // 2 + 1)

        def s_full(item):
            return full[item[0]][item[1] % 2]

        def s_free(item):
            return free[item[0]][item[1] % 2]

        d_x = [sem(f"d_x{g}") for g in range(G)]
        d_cst, d_ids, d_permc = sem("d_cst"), sem("d_ids"), sem("d_permc")
        d_w = {n: sem(f"d_{n}") for n in ("wq", "wk", "wv", "wo", "w2")}
        d_wq2 = sem("d_wq2")
        d_lora, d_up, d_dn, d_wg = sem("d_lora"), sem("d_up"), sem("d_dn"), [sem(f"d_wg{g}") for g in range(G)]
        d_out = [sem(f"d_out{g}") for g in range(G)]
        idx_ready = sem("idx_ready")
        setup = sem("setup")
        wbd_ready = sem("wbd_ready")
        vz_zero = sem("vz_zero")
        prep_hi = sem("prep_hi")
        pick_ready, up_hi, up_ready = sem("pick_ready"), sem("up_hi"), sem("up_ready")
        bs_hi, bs_ready = sem("bs_hi"), sem("bs_ready")
        xc_hi = sem("xc_hi")
        rot_shuf, rot_sin, roped = sem("rot_shuf"), sem("rot_sin"), sem("roped")
        kbd_v, kbd_p, scored = sem("kbd_v"), sem("kbd_p"), sem("scored")
        maxed, shifted, exped = sem("maxed"), sem("shifted"), sem("exped")
        summed, recip, normed, turned = sem("summed"), sem("recip"), sem("normed"), sem("turned")
        pbd_v, pbd_a, pv_done = sem("pbd_v"), sem("pbd_a"), sem("pv_done")
        o_hi = sem("o_hi")
        x1_hi = sem("x1_hi")
        gstep, gex_ready = sem("gstep"), sem("gex_ready")
        gap, gexp = sem("gap"), sem("gexp")
        hg_hi, hg_ready = sem("hg_hi"), sem("hg_ready")
        x2_hi = sem("x2_hi")
        downed = sem("downed")
        y_hi = sem("y_hi")

        x_d = x.rearrange("(g t b) c d -> g (b c) t d", g=G, t=GT)
        out_d = out.rearrange("(g t b) c d -> g (b c) t d", g=G, t=GT)
        w_d = {"wq": wq, "wk": wk, "wv": wv, "wo": wo}
        block = ctx.enter_context(nc.Block())

        @block.sync
        def _(sp):
            def load_x(g):
                sp.dma_start(xs[:, g % XS, :, :], x_d[g]).then_inc(d_x[g], 16)

            def load_w(name, dst):
                sp.dma_start(dst, w_d[name].rearrange("(c p) k -> p c k", p=P)).then_inc(d_w[name], 16)

            sp.dma_start(cst[:, :], consts).then_inc(d_cst, 16)
            wq_rows = wq.rearrange("(c p) k -> p c k", p=P)
            for h, landed in ((slice(0, D // 2), d_w["wq"]), (slice(D // 2, D), d_wq2)):
                sp.dma_start(raw_q[:, :, h], wq_rows[:, :, h]).then_inc(landed, 16)
            load_x(0)
            with nc.allow_non_contiguous_dma(reason="512 indices, once"):
                sp.dma_start(permc[:, :], perm.rearrange("(c p) -> p c", p=P)).then_inc(d_permc, 16)
            sp.wait_ge(d_wg[0], 16 * GT)
            load_w("wk", raw_k)
            load_w("wv", raw_v)
            load_w("wo", raw_o)
            wait_prep(sp, "wq")
            sp.dma_start(raw_a, wa.rearrange("e r d -> (e r) d")).then_inc(d_lora, 16)
            for c in range(KC):
                sp.dma_start(raw_b[:, c, :, :], wb[:, P * c:P * c + P, :].rearrange("e p r -> p e r")
                             ).then_inc(d_lora, 16)
            sp.dma_start(raw_r[0:E, :], wr).then_inc(d_lora, 16)
            sp.dma_start(raw_p, perm.partition_broadcast(P)).then_inc(d_lora, 16)
            for j in range(4):
                sp.dma_start(raw_up[FD * j:FD * j + FD, :, :],
                             up.rearrange("(c j) d m -> j d c m", j=4)[j]).then_inc(d_up, 16)
            sp.dma_start(dn[:, :, :], down.rearrange("h m d -> m h d")).then_inc(d_dn, 16)
            wait_prep(sp, "wo")
            load_x(1)
            load_x(2)
            for g in range(G):
                for t in range(GT):
                    wait_read(sp, Dd(g, UN + t))
                    if g == G - 1:
                        sp.dma_start(out_d[g, :, t, :], xs[:, g % XS, t, :]).then_inc(d_out[g], 16)
                if g < G - 1:
                    sp.dma_start(out_d[g], xs[:, g % XS, :, :]).then_inc(d_out[g], 16)
                if g + XS < G:
                    sp.wait_ge(d_out[g], 16)
                    load_x(g + XS)
            for g in range(G):
                sp.wait_ge(d_out[g], 16 * GT if g == G - 1 else 16)

        @block.gpsimd
        def _(pool):
            pool.memset(vz[:, :, :, :], 0.0).then_inc(vz_zero, 1)
            pool.wait_ge(idx_ready, 1)
            for t in range(TILES):
                pool.indirect_dma_start(out=wg[:, t, :], out_offset=None,
                                        in_=wcond.rearrange("s c d -> (s c) d"),
                                        in_offset=bass.IndirectOffsetOnAxis(ap=idx[:, t:t + 1], axis=0)
                                        ).then_inc(d_wg[t // GT], 16)
            pool.wait_ge(d_permc, 16)
            wait_prep(pool, "wk")
            for c in range(KC):
                pool.indirect_dma_start(out=raw_w2[:, c, :], out_offset=None, in_=w2,
                                        in_offset=bass.IndirectOffsetOnAxis(
                                            ap=permc[:, c:c + 1].bitcast(U32), axis=0)
                                        ).then_inc(d_w["w2"], 16)

            def rope(g, i):
                n = 4 * g + i
                dst = (qr, kr)[i // 2][:, 2 * (i % 2):2 * (i % 2) + 2, :].rearrange("p c (b d) -> p (c b) d", d=T)
                rv = rot[:, :, :].rearrange("p c (b d) -> p (c b) d", d=T)
                pool.wait_ge(rot_shuf, n + 1)
                pool.tensor_tensor(rv, rv, con("sin").unsqueeze(1).to_broadcast([P, 2 * N // T, T]),
                                   ALU.mult).then_inc(rot_sin, 1)
                pool.wait_ge(rot_sin, n + 1)
                wait_read(pool, A(g, (Q, K_)[i // 2] + i % 2))
                pool.tensor_tensor(dst, dst, rv, ALU.add).then_inc(roped, 1)

            def k_blocks(g, t, c):
                n = 8 * g + 4 * t + c
                pool.wait_ge(roped, 4 * g + (4 if c >= 2 else 3))
                if n >= KC:
                    wait_scored(pool, n - KC)
                kv = kr[:, c, P * t:P * t + P].rearrange("p (b s) -> p b s", b=BT)
                pool.tensor_tensor(
                    kbd[:, c, :, :].rearrange("p b (h s) -> p b h s", h=HC),
                    kv.unsqueeze(2).to_broadcast([P, BT, HC, T]),
                    con("head").unsqueeze(1).unsqueeze(3).to_broadcast([P, BT, HC, T]),
                    ALU.mult).then_inc(kbd_p, 1)

            def shift(g, i):
                n = 4 * g + i
                pool.wait_ge(maxed, n + 1)
                pool.tensor_tensor(pr[:, i, :, :], pr[:, i, :, :],
                                   mx[:, i, :].unsqueeze(2).to_broadcast([P, NH // 2, T]),
                                   ALU.subtract).then_inc(shifted, 1)

            def norm(g, i):
                n = 4 * g + i
                pool.wait_ge(recip, n + 1)
                pool.tensor_tensor(pr[:, i, :, :], pr[:, i, :, :],
                                   mx[:, i, :].unsqueeze(2).to_broadcast([P, NH // 2, T]),
                                   ALU.mult).then_inc(normed, 1)

            for i in range(4):
                rope(0, i)
            k_blocks(0, 0, 1)
            k_blocks(0, 0, 3)
            for g in range(G):
                k_blocks(g, 1, 1)
                shift(g, 0)
                shift(g, 1)
                k_blocks(g, 1, 3)
                shift(g, 2)
                shift(g, 3)
                norm(g, 0)
                if g == 0:
                    rope(1, 0)
                norm(g, 1)
                if g == 0:
                    rope(1, 1)
                elif g + 1 < G:
                    rope(g + 1, 0)
                norm(g, 2)
                norm(g, 3)
                if g + 1 < G:
                    for i in range(2 if g == 0 else 1, 4):
                        rope(g + 1, i)
                    k_blocks(g + 1, 0, 1)
                    k_blocks(g + 1, 0, 3)

        @block.tensor
        def _(pe):
            def mm3(dst, hi_l, lo_l, hi_r, lo_r, start, stop, skip=False):
                pe.matmul(dst, hi_l, hi_r, start=start, stop=False, skip_group_check=skip)
                pe.matmul(dst, hi_l, lo_r, start=False, stop=False, skip_group_check=skip)
                return pe.matmul(dst, lo_l, hi_r, start=False, stop=stop, skip_group_check=skip)

            def prep_w(name, raw):
                pe.wait_ge(d_w[name], 64 if name == "w2" else 16)
                if name == "wq":
                    pe.wait_ge(d_cst, 16)
                for k in range(KC):
                    if name == "wq" and k == KC // 2:
                        pe.wait_ge(d_wq2, 16)
                    it = prep(name, k)
                    wait_free(pe, it)
                    for c in range(KC):
                        last = pe.transpose(bank(it)[:, P * c:P * c + P], raw[:, c, P * k:P * k + P], ident)
                    last.then_inc(s_full(it), 1)

            def cond(g, t):
                pe.wait_ge(d_x[g], 16)
                pe.wait_ge(wbd_ready, g + 1)
                it = A(g, COND + t)
                wait_free(pe, it)
                for c in range(KC):
                    last = pe.matmul(bank(it)[:, P * c:P * c + P], xs[:, g % XS, t, P * c:P * c + P],
                                     wbd[:, t, :, :], start=True, stop=True)
                last.then_inc(s_full(it), 1)

            def qk(g, name, first, i):
                W = WT[name]
                if name == "wq" and i == 0:
                    for t in range(GT):
                        wait_read(pe, A(g, COND + t))
                it = A(g, first + i)
                wait_free(pe, it)
                for h in range(2):
                    c = 2 * i + h
                    for k in range(KC):
                        last = mm3(bank(it)[:, N * h:N * h + N],
                                   W[:, 0, k, P * c:P * c + P], W[:, 1, k, P * c:P * c + P],
                                   xc[:, 0, k, :], xc[:, 1, k, :], k == 0, k == KC - 1)
                last.then_inc(s_full(it), 1)

            def v(g, t):
                it = A(g, V + t)
                wait_free(pe, it)
                W = WT["wv"]
                for k in range(KC):
                    last = mm3(bank(it)[:, :], xc[:, 0, k, P * t:P * t + P], xc[:, 1, k, P * t:P * t + P],
                               W[:, 0, k, :], W[:, 1, k, :], k == 0, k == KC - 1)
                last.then_inc(s_full(it), 1)

            def scores(g, i):
                t, half = i // 2, i % 2
                it = S_scores(g, i)
                wait_free(pe, it)
                pe.wait_ge(roped, 4 * g + 4)
                for c in (2 * half, 2 * half + 1):
                    n = 8 * g + 4 * t + c
                    pe.wait_ge((kbd_v, kbd_p)[c % 2], n // 2 + 1)
                    for b in range(BT):
                        at = P * t + T * b
                        last = pe.matmul(bank(it)[T * b:T * b + T, N * (c % 2):N * (c % 2) + N],
                                         qr[:, c, at:at + T], kbd[:, c, b, :], start=True, stop=True)
                    last.then_inc(scored if c % 2 == 0 else s_full(it), 1)

            def pv(g, t, c):
                it = C(g, PV + t)
                if c == 0:
                    wait_free(pe, it)
                    wait_read(pe, A(g, V + t))
                n = 8 * g + 4 * t + c
                pe.wait_ge(pbd_v, n + 1)
                pe.wait_ge(pbd_a, n + 1)
                for e in range(2):
                    for j in range(4):
                        last = pe.matmul(bank(it)[32 * j:32 * j + 32, P * c:P * c + P],
                                         vz[:, t, 4 * c + j, HD * e:HD * e + 2 * HD],
                                         pbd[:, c % 2, 2 * j + e, :, :],
                                         start=(e == 0), stop=(e == 1), skip_group_check=True)
                last.then_inc(pv_done if c < KC - 1 else s_full(it), 1)

            def wo_proj(g, t):
                it = C(g, WO + t)
                wait_free(pe, it)
                wait_read(pe, C(g, PV + t))
                W, o = WT["wo"], attn_out(g)
                for k in range(KC):
                    last = mm3(bank(it)[:, :], o[:, 0, k, P * t:P * t + P], o[:, 1, k, P * t:P * t + P],
                               W[:, 0, k, :], W[:, 1, k, :], k == 0, k == KC - 1)
                last.then_inc(s_full(it), 1)

            def turn_x1(g, t):
                it = C(g, XT + t)
                wait_free(pe, it)
                wait_read(pe, C(g, WO + t))
                for c in range(KC):
                    last = pe.transpose(bank(it)[:, P * c:P * c + P], xs[:, g % XS, t, P * c:P * c + P], ident)
                last.then_inc(s_full(it), 1)

            def lora_down(g):
                it = C(g, LR)
                wait_free(pe, it)
                for t in range(GT):
                    wait_read(pe, C(g, XT + t))
                for k in range(KC):
                    last = mm3(bank(it)[0:E, 0:N], rT[:, 0, k, :], rT[:, 1, k, :],
                               x1[:, 0, k, :], x1[:, 1, k, :], k == 0, k == KC - 1)
                last.then_inc(s_full(it), 1)
                it = C(g, LH)
                wait_free(pe, it)
                for k in range(KC):
                    last = mm3(bank(it)[:, 0:N], aT[:, 0, k, :], aT[:, 1, k, :], x1[:, 0, k, :], x1[:, 1, k, :],
                               k == 0, k == KC - 1)
                last.then_inc(s_full(it), 1)

            def turn_logits(g):
                it = C(g, LT)
                wait_free(pe, it)
                wait_read(pe, C(g, LR))
                for t in range(GT):
                    last = pe.transpose(bank(it)[:, E * t:E * t + E], lg[:, P * t:P * t + P], ident[0:E, 0:E])
                last.then_inc(s_full(it), 1)

            def turn_gates(g):
                it = C(g, GTR)
                wait_free(pe, it)
                pe.wait_ge(gex_ready, g + 1)
                for t in range(GT):
                    last = pe.transpose(bank(it)[:, P * t:P * t + P],
                                        gex[:, t, :, :].rearrange("p e r -> p (e r)"), ident)
                last.then_inc(s_full(it), 1)

            def experts_base(g, c):
                it = Dd(g, W_ + c // 2)
                if c % 2 == 0:
                    wait_free(pe, it)
                W, h = WT["w2"], c % 2
                for k in range(KC):
                    mm3(bank(it)[:, N * h:N * h + N], W[:, 0, k, P * c:P * c + P], W[:, 1, k, P * c:P * c + P],
                        x1[:, 0, k, :], x1[:, 1, k, :], h == 0 and k == 0, False, skip=True)

            def experts_lora(g, i):
                it = Dd(g, W_ + i)
                pe.wait_ge(hg_ready, g + 1)
                for h in range(2):
                    c = 2 * i + h
                    last = mm3(bank(it)[:, N * h:N * h + N], bT[:, 0, P * c:P * c + P], bT[:, 1, P * c:P * c + P],
                               hg[:, 0, :], hg[:, 1, :], False, h == 1, skip=True)
                last.then_inc(s_full(it), 1)

            def ffn_up(g, i):
                it = Dd(g, UP + i)
                wait_free(pe, it)
                wait_read(pe, Dd(g, W_ + i // 4))
                c = i // 2
                for h in range(2):
                    j = 2 * (i % 2) + h
                    last = mm3(bank(it)[:, N * h:N * h + N], upP[:, 0, c, j, :], upP[:, 1, c, j, :],
                               y2[:, 0, c, :], y2[:, 1, c, :], True, True)
                last.then_inc(s_full(it), 1)

            def ffn_down(g, c):
                it = S_down(g, c // 2)
                if c % 2 == 0:
                    wait_free(pe, it)
                for i in range(2):
                    wait_read(pe, Dd(g, UP + 2 * c + i))
                for j in range(4):
                    last = pe.matmul(bank(it)[32 * j:32 * j + 32, N * (c % 2):N * (c % 2) + N],
                                     dn[:, 4 * c + j, :], act[:, (2 * c + j // 2) % 4, j % 2, :],
                                     start=True, stop=True)
                last.then_inc(downed if c % 2 == 0 else s_full(it), 1)

            def unpermute(g, t, halves=(0, 1)):
                it = Dd(g, UN + t)
                for i in halves:
                    if i == 0:
                        wait_free(pe, it)
                    wait_read(pe, S_down(g, i))
                    for c in (2 * i, 2 * i + 1):
                        for part in range(2):
                            last = pe.matmul(bank(it)[:, :], y2[:, part, c, P * t:P * t + P], unperm[:, c, :],
                                             start=(c == 0 and part == 0), stop=(c == KC - 1 and part == 1),
                                             skip_group_check=True)
                    if i == 1:
                        last.then_inc(s_full(it), 1)

            def ffn_first(g):
                for i in range(4):
                    ffn_up(g, i)
                ffn_down(g, 0)
                ffn_up(g, 4)
                ffn_up(g, 5)
                ffn_down(g, 1)

            def ffn_last(g):
                ffn_up(g, 6)
                ffn_up(g, 7)
                ffn_down(g, 2)
                ffn_down(g, 3)

            def prep_b():
                pe.wait_ge(bs_ready, 1)
                for part in range(2):
                    it = prep("b", part)
                    wait_free(pe, it)
                    for c in range(KC):
                        last = pe.matmul(bank(it)[:, :], bs[:, part, P * c:P * c + P],
                                         pick[:, c, :], start=(c == 0), stop=(c == KC - 1))
                    last.then_inc(s_full(it), 1)

            def prep_ar():
                for name, raw, n in (("a", raw_a, P), ("r", raw_r[0:E, :], E)):
                    it = prep(name)
                    wait_free(pe, it)
                    for k in range(KC):
                        last = pe.transpose(bank(it)[:, n * k:n * k + n], raw[:, P * k:P * k + P],
                                            ident[0:n, 0:n])
                    last.then_inc(s_full(it), 1)

            prep_w("wq", raw_q)
            cond(0, 0)
            cond(0, 1)
            prep_w("wk", raw_k)
            wait_prep(pe, "wq")
            qk(0, "wq", Q, 0)
            prep_w("wv", raw_v)
            qk(0, "wq", Q, 1)
            wait_prep(pe, "wk")
            qk(0, "wk", K_, 0)
            prep_w("wo", raw_o)
            qk(0, "wk", K_, 1)
            for k in range(KC):
                it = prep("unperm", k)
                wait_free(pe, it)
                for c in range(KC):
                    if k == 0:
                        pe.wait_ge(pick_ready, c + 1)
                    last = pe.transpose(bank(it)[:, P * c:P * c + P], pick[:, c, P * k:P * k + P].bitcast(F32), ident)
                last.then_inc(s_full(it), 1)
            prep_w("w2", raw_w2)
            prep_b()
            wait_prep(pe, "wv")
            v(0, 0)
            scores(0, 0)
            scores(0, 1)
            prep_ar()
            wait_prep(pe, "wo")
            v(0, 1)
            cond(1, 0)
            cond(1, 1)
            for g in range(G):
                if g:
                    if g + 1 < G:
                        cond(g + 1, 0)
                    turn_x1(g - 1, 1)
                    scores(g, 0)
                    scores(g, 1)
                    lora_down(g - 1)
                    turn_logits(g - 1)
                scores(g, 2)
                if g:
                    for c in range(KC - 1):
                        experts_base(g - 1, c)
                    if g + 1 < G:
                        cond(g + 1, 1)
                    turn_gates(g - 1)
                    experts_base(g - 1, KC - 1)
                    experts_lora(g - 1, 0)
                    experts_lora(g - 1, 1)
                scores(g, 3)
                if g:
                    ffn_first(g - 1)
                    if g + 1 < G:
                        ffn_last(g - 1)
                if g == 0:
                    qk(1, "wq", Q, 0)
                    qk(1, "wq", Q, 1)
                    qk(1, "wk", K_, 0)
                    pv(0, 0, 0)
                    pv(0, 0, 1)
                    qk(1, "wk", K_, 1)
                    pv(0, 0, 2)
                    v(1, 0)
                    pv(0, 0, 3)
                    pv(0, 1, 0)
                    v(1, 1)
                    pv(0, 1, 1)
                    pv(0, 1, 2)
                    wo_proj(0, 0)
                    pv(0, 1, 3)
                elif g + 1 < G:
                    qk(g + 1, "wq", Q, 0)
                    pv(g, 0, 0)
                    unpermute(g - 1, 0)
                    pv(g, 0, 1)
                    unpermute(g - 1, 1)
                    pv(g, 0, 2)
                    qk(g + 1, "wq", Q, 1)
                    pv(g, 0, 3)
                    qk(g + 1, "wk", K_, 0)
                    pv(g, 1, 0)
                    qk(g + 1, "wk", K_, 1)
                    pv(g, 1, 1)
                    v(g + 1, 0)
                    pv(g, 1, 2)
                    pv(g, 1, 3)
                    wo_proj(g, 0)
                    v(g + 1, 1)
                else:
                    ffn_up(g - 1, 6)
                    ffn_up(g - 1, 7)
                    pv(g, 0, 0)
                    ffn_down(g - 1, 2)
                    pv(g, 0, 1)
                    ffn_down(g - 1, 3)
                    pv(g, 0, 2)
                    pv(g, 0, 3)
                    unpermute(g - 1, 0, (0,))
                    wo_proj(g, 0)
                    pv(g, 1, 0)
                    unpermute(g - 1, 0, (1,))
                    pv(g, 1, 1)
                    turn_x1(g, 0)
                    pv(g, 1, 2)
                    pv(g, 1, 3)
                    unpermute(g - 1, 1, (0,))
                    wo_proj(g, 1)
                if g + 1 < G:
                    turn_x1(g, 0)
                    wo_proj(g, 1)
                if g == 0:
                    wait_prep(pe, "r", 1)
                    pe.wait_ge(up_ready, 4)
                    wait_prep(pe, "unperm")
                    pe.wait_ge(d_dn, 16)
            turn_x1(G - 1, 1)
            unpermute(G - 2, 1, (1,))
            lora_down(G - 1)
            turn_logits(G - 1)
            for c in range(KC - 1):
                experts_base(G - 1, c)
            turn_gates(G - 1)
            experts_base(G - 1, KC - 1)
            experts_lora(G - 1, 0)
            experts_lora(G - 1, 1)
            ffn_first(G - 1)
            ffn_last(G - 1)
            for half in range(2):
                for t in range(GT):
                    unpermute(G - 1, t, (half,))

        @block.scalar
        def _(sc):
            def copy(dst, src):
                return sc.activation(dst, src, ACT.Copy)

            def prep_his(name, n, dst):
                for k in range(n):
                    it = prep(name, k)
                    wait_full(sc, it)
                    copy(dst(k), bank(it)[:, 0:dst(k).free_size()]).then_inc(prep_hi, 1)

            def cond_hi(g, t):
                it = A(g, COND + t)
                wait_full(sc, it)
                copy(xc[:, 0, :, P * t:P * t + P], bank(it)[:, :].rearrange("p (c n) -> p c n", c=KC)
                     ).then_inc(xc_hi, 1)

            def v_out(g, t):
                it = A(g, V + t)
                if g == 0 and t == 0:
                    sc.wait_ge(vz_zero, 1)
                wait_full(sc, it)
                dst = vz[:, t, :, :].rearrange("p q (s f) -> p q s f", f=HD)[:, :, 0:3:2, :]
                copy(dst, bank(it)[:, :].rearrange("p (q s f) -> p q s f", s=2, f=HD)).then_inc(s_free(it), 1)

            def exp(g, i):
                sc.wait_ge(shifted, 4 * g + i + 1)
                sc.activation(pr[:, i, :, :], pr[:, i, :, :], ACT.Exp, scale=float(HD) ** -0.5
                              ).then_inc(exped, 1)

            def gate_exp(g):
                sc.wait_ge(gap, g + 1)
                sc.activation(e2, e2, ACT.Exp).then_inc(gexp, 1)

            def gelu_table(g):
                sc.activation(unused[:, g:g + 1], con("pos"), ACT.Gelu)

            def h_out(g):
                it = C(g, LH)
                wait_full(sc, it)
                copy(hs, bank(it)[:, 0:N]).then_inc(s_free(it), 1)

            def probs_block(g, t, c):
                n = 8 * g + 4 * t + c
                sc.wait_ge(turned, 4 * g + 2 * t + c // 2 + 1)
                if n >= 2:
                    wait_pv(sc, n - 2)
                if n == 0:
                    wait_prep(sc, "r", 1)
                src = pT(2 * t + c // 2)[:, HC * (c % 2):HC * (c % 2) + HC, :]
                b = BT - 1
                sc.activation(pbd[:, c % 2, :, b, :], src, ACT.Copy, scale=con("seq")[:, b:b + 1]
                              ).then_inc(pbd_a, 1)

            def split_hi(it, dst, s):
                wait_full(sc, it)
                copy(dst, bank(it)[:, :].rearrange("p (c n) -> p c n", n=dst.shape[-1])).then_inc(s, 1)

            def gelu(g, i):
                it = Dd(g, UP + i)
                n = 8 * g + i
                wait_full(sc, it)
                if n >= 4:
                    wait_down(sc, (n - 4) // 8, (n - 4) % 8 // 2)
                sc.activation(act[:, i % 4, :, :], bank(it)[:, :].rearrange("p (h n) -> p h n", h=2), ACT.Gelu
                              ).then_inc(s_free(it), 1)

            def x2_his(g):
                for i in range(2):
                    split_hi(Dd(g, W_ + i), y2[:, 0, 2 * i:2 * i + 2, :], x2_hi)

            def ffn(g):
                last = g == G - 2
                for i in range(6):
                    gelu(g, i)
                if last:
                    probs_block(g + 1, 0, 0)
                    gelu(g, 6)
                    gelu(g, 7)
                    probs_block(g + 1, 0, 1)
                    probs_block(g + 1, 0, 2)
                    probs_block(g + 1, 0, 3)
                    split_hi(S_down(g, 0), y2[:, 0, 0:2, :], y_hi)
                    exp(g + 1, 2)
                    exp(g + 1, 3)
                    split_hi(C(g + 1, PV), attn_out(g + 1)[:, 0, :, 0:P], o_hi)
                    split_hi(S_down(g, 1), y2[:, 0, 2:4, :], y_hi)
                    probs_block(g + 1, 1, 0)
                    probs_block(g + 1, 1, 1)
                    probs_block(g + 1, 1, 2)
                    probs_block(g + 1, 1, 3)
                else:
                    split_hi(S_down(g, 0), y2[:, 0, 0:2, :], y_hi)
                    gelu(g, 6)
                    gelu(g, 7)
                    if g + 1 < G:
                        probs_block(g + 1, 0, 0)
                        probs_block(g + 1, 0, 1)
                    split_hi(S_down(g, 1), y2[:, 0, 2:4, :], y_hi)

            sc.dma_start(ids[:, 0, :], subj.partition_broadcast(P)).then_inc(d_ids, 16)
            sc.dma_start(ids[:, 1, :], lang.partition_broadcast(P)).then_inc(d_ids, 16)
            prep_his("wq", KC, lambda k: WT["wq"][:, 0, k, :])
            cond_hi(0, 0)
            cond_hi(0, 1)
            prep_his("wk", KC, lambda k: WT["wk"][:, 0, k, :])
            prep_his("wv", KC, lambda k: WT["wv"][:, 0, k, :])
            sc.wait_ge(d_up, 64)
            for j in range(4):
                sc.activation(upP[:, 0, :, j, :], raw_up, ACT.Copy, scale=con("seq")[:, j:j + 1]
                              ).then_inc(up_hi, 1)
            prep_his("wo", KC, lambda k: WT["wo"][:, 0, k, :])
            sc.wait_ge(d_lora, 16 * (3 + KC))
            copy(bs[:, 0, :], raw_q[:, 1, :]).then_inc(bs_hi, 1)
            for k in range(KC):
                it = prep("unperm", k)
                wait_full(sc, it)
                copy(unperm[:, k, :], bank(it)[:, :]).then_inc(s_free(it), 1)
            prep_his("w2", KC, lambda k: WT["w2"][:, 0, k, :])
            wait_full(sc, prep("b", 0))
            copy(bT[:, 0, :], bank(prep("b", 0))[:, :]).then_inc(s_free(prep("b", 0)), 1)
            v_out(0, 0)
            prep_his("a", 1, lambda k: aT[:, 0, :, :].rearrange("p a b -> p (a b)"))
            prep_his("r", 1, lambda k: rT[:, 0, :, :].rearrange("p a b -> p (a b)"))
            v_out(0, 1)
            cond_hi(1, 0)
            cond_hi(1, 1)
            for g in range(G):
                if g:
                    h_out(g - 1)
                exp(g, 0)
                exp(g, 1)
                if g:
                    gate_exp(g - 1)
                    gelu_table(g - 1)
                    if g + 1 < G:
                        cond_hi(g + 1, 1)
                    x2_his(g - 1)
                    ffn(g - 1)
                if g + 1 < G:
                    exp(g, 2)
                    exp(g, 3)
                    if g == 0:
                        probs_block(g, 0, 0)
                        probs_block(g, 0, 1)
                    probs_block(g, 0, 2)
                    probs_block(g, 0, 3)
                if g < G - 1:
                    probs_block(g, 1, 0)
                    split_hi(C(g, PV), attn_out(g)[:, 0, :, 0:P], o_hi)
                    probs_block(g, 1, 1)
                    probs_block(g, 1, 2)
                    probs_block(g, 1, 3)
                if g + 1 < G:
                    v_out(g + 1, 0)
                split_hi(C(g, PV + 1), attn_out(g)[:, 0, :, P:2 * P], o_hi)
                if g + 1 < G:
                    v_out(g + 1, 1)
                split_hi(C(g, XT), x1[:, 0, :, 0:P], x1_hi)
                if g + 2 < G:
                    cond_hi(g + 2, 0)
                split_hi(C(g, XT + 1), x1[:, 0, :, P:2 * P], x1_hi)
            h_out(G - 1)
            gate_exp(G - 1)
            gelu_table(G - 1)
            x2_his(G - 1)
            ffn(G - 1)

        @block.vector
        def _(ve):
            steps = [0]

            def step(ins):
                steps[0] += 1
                ins.then_inc(setup, 1)
                ve.wait_ge(setup, steps[0])

            def split_lo(it, hi, lo, s_hi, n_hi):
                ve.wait_ge(s_hi, n_hi)
                src = bank(it)[:, 0:hi.free_size()]
                if len(hi.shape) == 3:
                    src = src.rearrange("p (c n) -> p c n", n=hi.shape[-1])
                wait_full(ve, it)
                ve.tensor_tensor(lo, src, hi.bitcast(F32), ALU.subtract).then_inc(s_free(it), 1)

            def prep_los(name, n, w):
                his = PREP[name] - sum(n for w, n in (("unperm", KC), ("b", 2)) if PREP[name] > PREP[w])
                for k in range(n):
                    it = prep(name, k)
                    split_lo(it, w(k, 0), w(k, 1), prep_hi, his + k + 1)

            def cond_lo(g, t):
                at = slice(P * t, P * t + P)
                split_lo(A(g, COND + t), xc[:, 0, :, at], xc[:, 1, :, at], xc_hi, GT * g + t + 1)

            def blocks(g):
                ve.wait_ge(d_wg[g], 16 * GT)
                if g:
                    wait_full(ve, A(g - 1, COND + 1))
                for b in range(BT):
                    i = ve.tensor_scalar(wbd[:, :, b, :], wg[:, GT * g:GT * g + GT, :],
                                         con("seq")[:, b:b + 1], None, ALU.mult)
                i.then_inc(wbd_ready, 1)

            def rope(g, i):
                n = 4 * g + i
                it = A(g, (Q, K_)[i // 2] + i % 2)
                dst = (qr, kr)[i // 2][:, 2 * (i % 2):2 * (i % 2) + 2, :].rearrange("p c (b d) -> p (c b) d", d=T)
                src = bank(it)[:, :]
                wait_full(ve, it)
                if n:
                    ve.wait_ge(roped, n)
                half = HD // 2
                order = [(j + half) if j % HD < half else (j - half) for j in range(32)]
                ve.stream_shuffle(rot[:, :, :].rearrange("p c n -> p (c n)"), src, order).then_inc(rot_shuf, 1)
                ve.tensor_tensor(dst, src.rearrange("p (c d) -> p c d", d=T),
                                 con("cos").unsqueeze(1).to_broadcast([P, 2 * N // T, T]), ALU.mult
                                 ).then_inc(s_free(it), 1)

            def k_blocks(g, t, c):
                n = 8 * g + 4 * t + c
                ve.wait_ge(roped, 4 * g + (4 if c >= 2 else 3))
                if n >= KC:
                    wait_scored(ve, n - KC)
                kv = kr[:, c, P * t:P * t + P].rearrange("p (b s) -> p b s", b=BT)
                ve.tensor_tensor(
                    kbd[:, c, :, :].rearrange("p b (h s) -> p b h s", h=HC),
                    kv.unsqueeze(2).to_broadcast([P, BT, HC, T]),
                    con("head").unsqueeze(1).unsqueeze(3).to_broadcast([P, BT, HC, T]),
                    ALU.mult).then_inc(kbd_v, 1)

            def mask(g, i):
                it = S_scores(g, i)
                n = 4 * g + i
                wait_full(ve, it)
                if n == 0:
                    wait_prep(ve, "b", 1)
                ve.tensor_tensor(pr[:, i, :, :], bank(it)[:, :].rearrange("p (h s) -> p h s", s=T),
                                 con("causal").unsqueeze(1).to_broadcast([P, NH // 2, T]), ALU.add
                                 ).then_inc(s_free(it), 1)

            def row_max(g, i):
                wait_read(ve, S_scores(g, i))
                ve.tensor_reduce(mx[:, i, :], pr[:, i, :, :], AX_X, ALU.max).then_inc(maxed, 1)

            def mask_max(g, i):
                mask(g, i)
                row_max(g, i)

            def sums(g, i):
                n = 4 * g + i
                ve.wait_ge(exped, n + 1)
                ve.tensor_reduce(sm[:, i, :], pr[:, i, :, :], AX_X, ALU.add).then_inc(summed, 1)
                ve.wait_ge(summed, n + 1)
                ve.reciprocal(mx[:, i, :], sm[:, i, :]).then_inc(recip, 1)

            def turn(g, i):
                ve.wait_ge(normed, 4 * g + i + 1)
                if i:
                    ve.wait_ge(turned, 4 * g + i)
                ve.transpose(pT(i), pr[:, i, :, :]).then_inc(turned, 1)

            def probs_blocks(g, t, c):
                n = 8 * g + 4 * t + c
                ve.wait_ge(turned, 4 * g + 2 * t + c // 2 + 1)
                if n >= 2:
                    wait_pv(ve, n - 2)
                if n == 0:
                    wait_prep(ve, "r", 1)
                src = pT(2 * t + c // 2)[:, HC * (c % 2):HC * (c % 2) + HC, :]
                for b in range(BT - 1):
                    i = ve.tensor_scalar(pbd[:, c % 2, :, b, :], src, con("seq")[:, b:b + 1], None, ALU.mult)
                i.then_inc(pbd_v, 1)

            def o_lo(g, t):
                at = slice(P * t, P * t + P)
                o = attn_out(g)
                split_lo(C(g, PV + t), o[:, 0, :, at], o[:, 1, :, at], o_hi, GT * g + t + 1)

            def add_x(g, t):
                it = C(g, WO + t)
                wait_full(ve, it)
                ve.tensor_tensor(xs[:, g % XS, t, :], bank(it)[:, :], xs[:, g % XS, t, :], ALU.add
                                 ).then_inc(s_free(it), 1)

            def x1_lo(g, t):
                at = slice(P * t, P * t + P)
                split_lo(C(g, XT + t), x1[:, 0, :, at], x1[:, 1, :, at], x1_hi, GT * g + t + 1)

            def logits_out(g):
                it = C(g, LR)
                wait_full(ve, it)
                ve.tensor_copy(lg, bank(it)[0:E, 0:N]).then_inc(s_free(it), 1)

            gsteps = [0]

            def gate(ins):
                gsteps[0] += 1
                ins.then_inc(gstep, 1)
                ve.wait_ge(gstep, gsteps[0])

            def gates(g):
                it = C(g, LT)
                wide = [P, GT, E]

                def w(v):
                    return v.unsqueeze(2).to_broadcast(wide)

                experts_, experts16 = (con(n).unsqueeze(1).to_broadcast(wide) for n in ("expert", "expert16"))
                wait_full(ve, it)
                ve.tensor_tensor(L, bank(it)[:, 0:GT * E].rearrange("p (t e) -> p t e", t=GT),
                                 bias[:, GT * g:GT * g + GT, :], ALU.add).then_inc(s_free(it), 1)
                wait_read(ve, it)
                for src, m, oh in ((L, m1, oh1), (L2, m2, oh2)):
                    gate(ve.tensor_reduce(m, src, AX_X, ALU.max))
                    gate(ve.tensor_tensor(eq, src, w(m), ALU.is_equal))
                    gate(ve.scalar_tensor_tensor(out=cand, in0=eq, scalar=-16.0, in1=experts16,
                                                 op0=ALU.mult, op1=ALU.add))
                    gate(ve.tensor_reduce(i1, cand, AX_X, ALU.min))
                    gate(ve.tensor_tensor(oh, experts_, w(i1), ALU.is_equal))
                    if oh is oh1:
                        gate(ve.scalar_tensor_tensor(out=L2, in0=oh1, scalar=NEVER, in1=L,
                                                     op0=ALU.mult, op1=ALU.add))
                ve.tensor_tensor(e2, m2, m1, ALU.subtract).then_inc(gap, 1)
                ve.wait_ge(gexp, g + 1)
                gate(ve.tensor_scalar(g2, e2, 1.0, None, ALU.add))
                gate(ve.reciprocal(g1, g2))
                gate(ve.tensor_tensor(g2, e2, g1, ALU.mult))
                gate(ve.tensor_tensor(oh1, oh1, w(g1), ALU.mult))
                gate(ve.tensor_tensor(oh2, oh2, w(g2), ALU.mult))
                gate(ve.tensor_tensor(cand, oh1, oh2, ALU.add))
                ve.tensor_scalar(gex, cand.unsqueeze(3).to_broadcast([P, GT, E, R]), SCALING, None,
                                 ALU.mult).then_inc(gex_ready, 1)

            def gate_h(g):
                it = C(g, GTR)
                wait_full(ve, it)
                wait_read(ve, C(g, LH))
                ve.tensor_tensor(hgf, bank(it)[:, 0:N], hs, ALU.mult).then_inc(s_free(it), 1)
                wait_read(ve, it)
                ve.tensor_copy(hg[:, 0, :], hgf).then_inc(hg_hi, 1)
                ve.wait_ge(hg_hi, g + 1)
                ve.tensor_tensor(hg[:, 1, :], hgf, hg[:, 0, :].bitcast(F32), ALU.subtract).then_inc(hg_ready, 1)

            def x2_lo(g, i):
                at = slice(2 * i, 2 * i + 2)
                split_lo(Dd(g, W_ + i), y2[:, 0, at, :], y2[:, 1, at, :], x2_hi, 2 * g + i + 1)

            def y_lo(g, i):
                at = slice(2 * i, 2 * i + 2)
                split_lo(S_down(g, i), y2[:, 0, at, :], y2[:, 1, at, :], y_hi, 2 * g + i + 1)

            def add_ffn(g, t):
                it = Dd(g, UN + t)
                wait_full(ve, it)
                ve.tensor_tensor(xs[:, g % XS, t, :], bank(it)[:, :], xs[:, g % XS, t, :], ALU.add
                                 ).then_inc(s_free(it), 1)

            ve.wait_ge(d_ids, 32)
            ve.wait_ge(d_cst, 16)
            for b in range(BT):
                at = slice(T * b, T * b + T)
                i = ve.tensor_scalar(idx[at, :], ids[at, 0, b:B:BT], float(T), con("pos")[at, :],
                                     ALU.mult, ALU.add)
            i.then_inc(idx_ready, 1)
            for b in range(BT):
                at = slice(T * b, T * b + T)
                i = ve.tensor_copy(langf[at, :], ids[at, 1, b:B:BT])
            step(i)
            step(ve.tensor_tensor(bias, con("expert").unsqueeze(1).to_broadcast([P, TILES, E]),
                                  langf.unsqueeze(2).to_broadcast([P, TILES, E]), ALU.is_equal))
            step(ve.tensor_scalar(bias, bias, LANG_BIAS, None, ALU.mult))
            blocks(0)
            prep_los("wq", KC, lambda k, s: WT["wq"][:, s, k, :])
            cond_lo(0, 0)
            cond_lo(0, 1)
            prep_los("wk", KC, lambda k, s: WT["wk"][:, s, k, :])
            blocks(1)
            rope(0, 0)
            prep_los("wv", KC, lambda k, s: WT["wv"][:, s, k, :])
            ve.wait_ge(d_lora, 16 * (3 + KC))
            for c in range(KC):
                ve.tensor_scalar(pick[:, c, :], raw_p, con("row")[:, c:c + 1], None, ALU.is_equal
                                 ).then_inc(pick_ready, 1)
            rope(0, 1)
            rope(0, 2)
            prep_los("wo", KC, lambda k, s: WT["wo"][:, s, k, :])
            rope(0, 3)
            ve.wait_ge(bs_hi, 1)
            ve.tensor_tensor(bs[:, 1, :], raw_q[:, 1, :], bs[:, 0, :].bitcast(F32), ALU.subtract
                             ).then_inc(bs_ready, 1)
            prep_los("w2", KC, lambda k, s: WT["w2"][:, s, k, :])
            k_blocks(0, 0, 0)
            k_blocks(0, 0, 2)
            wait_full(ve, prep("b", 1))
            ve.tensor_copy(bT[:, 1, :], bank(prep("b", 1))[:, :]).then_inc(s_free(prep("b", 1)), 1)
            for g in range(G):
                mask_max(g, 0)
                k_blocks(g, 1, 0)
                if g:
                    logits_out(g - 1)
                mask_max(g, 1)
                if g == 0:
                    k_blocks(0, 1, 2)
                    prep_los("a", 1, lambda k, s: aT[:, s, :, :].rearrange("p a b -> p (a b)"))
                    prep_los("r", 1, lambda k, s: rT[:, s, :, :].rearrange("p a b -> p (a b)"))
                    cond_lo(1, 0)
                    cond_lo(1, 1)
                if g:
                    gates(g - 1)
                    gate_h(g - 1)
                    k_blocks(g, 1, 2)
                    x2_lo(g - 1, 0)
                    x2_lo(g - 1, 1)
                mask_max(g, 2)
                if g and g + 1 < G:
                    cond_lo(g + 1, 1)
                mask_max(g, 3)
                if g and g + 2 < G:
                    blocks(g + 2)
                sums(g, 0)
                if g == 0:
                    rope(1, 0)
                    sums(g, 1)
                    turn(g, 0)
                    probs_blocks(g, 0, 0)
                    probs_blocks(g, 0, 1)
                    rope(1, 1)
                    turn(g, 1)
                    sums(g, 2)
                    sums(g, 3)
                    probs_blocks(g, 0, 2)
                    rope(1, 2)
                    probs_blocks(g, 0, 3)
                    turn(g, 2)
                    turn(g, 3)
                    probs_blocks(g, 1, 0)
                    rope(1, 3)
                    o_lo(g, 0)
                    probs_blocks(g, 1, 1)
                    blocks(2)
                    probs_blocks(g, 1, 2)
                    probs_blocks(g, 1, 3)
                    for j in range(4):
                        ve.wait_ge(up_hi, j + 1)
                        ve.scalar_tensor_tensor(out=upP[:, 1, :, j, :], in0=raw_up, scalar=con("seq")[:, j:j + 1],
                                                in1=upP[:, 0, :, j, :].bitcast(F32), op0=ALU.mult, op1=ALU.subtract
                                                ).then_inc(up_ready, 1)
                elif g + 1 < G:
                    sums(g, 1)
                    turn(g, 0)
                    turn(g, 1)
                    probs_blocks(g, 0, 0)
                    y_lo(g - 1, 0)
                    probs_blocks(g, 0, 1)
                    y_lo(g - 1, 1)
                    rope(g + 1, 0)
                    probs_blocks(g, 0, 2)
                    sums(g, 2)
                    sums(g, 3)
                    probs_blocks(g, 0, 3)
                    add_ffn(g - 1, 0)
                    turn(g, 2)
                    turn(g, 3)
                    add_ffn(g - 1, 1)
                    rope(g + 1, 1)
                    probs_blocks(g, 1, 0)
                    rope(g + 1, 2)
                    o_lo(g, 0)
                    probs_blocks(g, 1, 1)
                    probs_blocks(g, 1, 2)
                    rope(g + 1, 3)
                    probs_blocks(g, 1, 3)
                else:
                    sums(g, 1)
                    turn(g, 0)
                    probs_blocks(g, 0, 0)
                    turn(g, 1)
                    probs_blocks(g, 0, 1)
                    probs_blocks(g, 0, 2)
                    probs_blocks(g, 0, 3)
                    y_lo(g - 1, 0)
                    sums(g, 2)
                    o_lo(g, 0)
                    sums(g, 3)
                    turn(g, 2)
                    probs_blocks(g, 1, 0)
                    y_lo(g - 1, 1)
                    turn(g, 3)
                    probs_blocks(g, 1, 1)
                    add_x(g, 0)
                    probs_blocks(g, 1, 2)
                    probs_blocks(g, 1, 3)
                if g + 1 < G:
                    add_x(g, 0)
                o_lo(g, 1)
                if g + 1 < G:
                    k_blocks(g + 1, 0, 0)
                    k_blocks(g + 1, 0, 2)
                x1_lo(g, 0)
                if g == G - 1:
                    add_ffn(g - 1, 0)
                add_x(g, 1)
                if g + 1 < G and g + 2 < G:
                    cond_lo(g + 2, 0)
                x1_lo(g, 1)
            add_ffn(G - 2, 1)
            logits_out(G - 1)
            gates(G - 1)
            gate_h(G - 1)
            x2_lo(G - 1, 0)
            x2_lo(G - 1, 1)
            y_lo(G - 1, 0)
            y_lo(G - 1, 1)
            add_ffn(G - 1, 0)
            add_ffn(G - 1, 1)


_INS = ["x", "itok_B_0_30", "itok_B_0_7", "L0_cond_weights", "L0_attn_wq", "L0_attn_wk", "L0_attn_wv",
        "L0_attn_wo", "L0_cond2_W", "L0_cond2_Wr", "L0_cond2_A", "L0_cond2_B", "L0_ffn_up", "L0_ffn_down",
        "L0_ffn_perm"]


def kernel(**inputs):
    import concourse.bacc as _bacc
    from concourse.bass_utils import run_bass_kernel_spmd as _run

    nc = _bacc.Bacc("TRN2", target_bir_lowering=False, num_devices=1,
                     dynamic_dma_scratch_size=4096)
    arrays, args = {}, []

    def give(name, a):
        a = np.ascontiguousarray(a)
        arrays[name] = a
        args.append(nc.dram_tensor(name, a.shape, mybir.dt.from_np(a.dtype), kind="ExternalInput").ap())

    for name in _INS:
        give(f"in_{name}", inputs[name])
    give("constants", constants())
    args.append(nc.dram_tensor("out_0", (B, T, D), F32, kind="ExternalOutput").ap())
    build(nc, *args)
    r = _run(nc, [arrays], core_ids=[0])
    return r.results[0]["out_0"]
```
